# Optimizing a Trainium2 kernel written in Bass

```python
import numpy as np
import jax
import jax.numpy as jnp

def _softmax(x, axis=-1):
    return jax.nn.softmax(x, axis=axis)

def _gelu(x):
    return jax.nn.gelu(x, approximate=True)

def _silu(x):
    return jax.nn.silu(x)

def _sigmoid(x):
    return jax.nn.sigmoid(x)

def _layernorm(x, axis=-1, eps=1e-05):
    m = jnp.mean(x, axis=axis, keepdims=True)
    v = jnp.var(x, axis=axis, keepdims=True)
    return (x - m) / jnp.sqrt(v + eps)

def _scatter_add(tgt, idx, src, axis=0):
    return tgt.at[idx].add(src)

def _segment_sum(src, seg, n):
    return jax.ops.segment_sum(src, seg, n)
kernel_name = 'mk_adaln_d2_jaxref_r8_84080a'

def setup_inputs(seed: int=0):
    np.random.seed(seed)
    _w = jnp.asarray

    def _L0_attn_setup():
        import jax, jax.numpy as jnp
        import numpy as np
        D_MODEL = 256
        NUM_HEADS = 16
        HEAD_DIM = D_MODEL // NUM_HEADS
        SCALE = HEAD_DIM ** (-0.5)
        ALPHA = 1.0
        key = jax.random.key(seed)
        ks = jax.random.split(key, 9)
        B, T = (2, 256)
        s = 0.02
        w = lambda k: jax.random.normal(k, (D_MODEL, D_MODEL), jnp.float32) * s
        b = lambda k: jax.random.normal(k, (D_MODEL,), jnp.float32) * s
        return {'x': jax.random.normal(ks[0], (B, T, D_MODEL), jnp.float32), 'q_w': w(ks[1]), 'q_b': b(ks[2]), 'k_w': w(ks[3]), 'k_b': b(ks[4]), 'v_w': w(ks[5]), 'v_b': b(ks[6]), 'o_w': w(ks[7]), 'o_b': b(ks[8])}
    _L0_attn_in = _L0_attn_setup()

    def _L0_ffn_setup():
        import jax, jax.numpy as jnp
        import numpy as np
        HIDDEN = 256
        INTER = 704
        B, S = (2, 256)

        def _ternary(key, shape):
            return jax.random.randint(key, shape, -1, 2).astype(jnp.float32)
        key = jax.random.key(seed)
        ks = jax.random.split(key, 7)
        x = jax.random.normal(ks[0], (B, S, HIDDEN), dtype=jnp.float32)
        gate_w = _ternary(ks[1], (INTER, HIDDEN))
        up_w = _ternary(ks[2], (INTER, HIDDEN))
        down_w = _ternary(ks[3], (HIDDEN, INTER))
        gate_s = jax.random.uniform(ks[4], (INTER,), minval=0.01, maxval=0.1, dtype=jnp.float32)
        up_s = jax.random.uniform(ks[5], (INTER,), minval=0.01, maxval=0.1, dtype=jnp.float32)
        down_s = jax.random.uniform(ks[6], (HIDDEN,), minval=0.01, maxval=0.1, dtype=jnp.float32)
        return {'x': x, 'gate_w': gate_w, 'up_w': up_w, 'down_w': down_w, 'gate_s': gate_s, 'up_s': up_s, 'down_s': down_s}
    _L0_ffn_in = _L0_ffn_setup()
    _L0_c = _w((lambda *s: np.random.randn(*s).astype(np.float32) * 0.05)(1, 256))
    _L0_wmod = _w((lambda *s: np.random.randn(*s).astype(np.float32) * 0.05)(256, 6 * 256) * 256 ** (-0.5))

    def _L1_attn_setup():
        import jax, jax.numpy as jnp
        import numpy as np
        EMBED_DIM = 256
        NUM_HEADS = 16
        HEAD_DIM = EMBED_DIM // NUM_HEADS
        SCALE = EMBED_DIM ** (-0.5)
        key = jax.random.key(seed)
        ks = jax.random.split(key, 9)
        d = EMBED_DIM
        s = 1.0 / np.sqrt(d)
        inp = {'x': jax.random.normal(ks[0], (2, 256, d), dtype=jnp.float32), 'wq': jax.random.uniform(ks[1], (d, d), jnp.float32, -s, s), 'bq': jnp.zeros((d,), jnp.float32), 'wk': jax.random.uniform(ks[2], (d, d), jnp.float32, -s, s), 'bk': jnp.zeros((d,), jnp.float32), 'wv': jax.random.uniform(ks[3], (d, d), jnp.float32, -s, s), 'bv': jnp.zeros((d,), jnp.float32), 'wo': jax.random.uniform(ks[4], (d, d), jnp.float32, -s, s), 'bo': jnp.zeros((d,), jnp.float32)}
        return inp
    _L1_attn_in = _L1_attn_setup()

    def _L1_ffn_setup():
        import jax, jax.numpy as jnp
        import numpy as np
        HIDDEN = 256
        N_EXPERTS = 8
        N_SHARED = 2
        TOP_K = 2
        MOE_FF = 176
        SHARED_FF = N_SHARED * MOE_FF
        SCALE = 2.5
        BATCH, SEQ = (2, 128)
        key = jax.random.key(seed)
        ks = jax.random.split(key, 8)
        s = 0.02
        return {'hidden_states': jax.random.normal(ks[0], (BATCH, SEQ, HIDDEN), jnp.float32), 'gate_w': jax.random.normal(ks[1], (N_EXPERTS, HIDDEN), jnp.float32) * s, 'shared_wg': jax.random.normal(ks[2], (SHARED_FF, HIDDEN), jnp.float32) * s, 'shared_wu': jax.random.normal(ks[3], (SHARED_FF, HIDDEN), jnp.float32) * s, 'shared_wd': jax.random.normal(ks[4], (HIDDEN, SHARED_FF), jnp.float32) * s, 'exp_wg': jax.random.normal(ks[5], (N_EXPERTS, MOE_FF, HIDDEN), jnp.float32) * s, 'exp_wu': jax.random.normal(ks[6], (N_EXPERTS, MOE_FF, HIDDEN), jnp.float32) * s, 'exp_wd': jax.random.normal(ks[7], (N_EXPERTS, HIDDEN, MOE_FF), jnp.float32) * s}
    _L1_ffn_in = _L1_ffn_setup()
    _L1_c = _w((lambda *s: np.random.randn(*s).astype(np.float32) * 0.05)(1, 256))
    _L1_wmod = _w((lambda *s: np.random.randn(*s).astype(np.float32) * 0.05)(256, 6 * 256) * 256 ** (-0.5))
    _d = {'L0_attn_x': _L0_attn_in['x'], 'L0_attn_q_w': _L0_attn_in['q_w'], 'L0_attn_q_b': _L0_attn_in['q_b'], 'L0_attn_k_w': _L0_attn_in['k_w'], 'L0_attn_k_b': _L0_attn_in['k_b'], 'L0_attn_v_w': _L0_attn_in['v_w'], 'L0_attn_v_b': _L0_attn_in['v_b'], 'L0_attn_o_w': _L0_attn_in['o_w'], 'L0_attn_o_b': _L0_attn_in['o_b'], 'L0_ffn_gate_w': _L0_ffn_in['gate_w'], 'L0_ffn_up_w': _L0_ffn_in['up_w'], 'L0_ffn_down_w': _L0_ffn_in['down_w'], 'L0_ffn_gate_s': _L0_ffn_in['gate_s'], 'L0_ffn_up_s': _L0_ffn_in['up_s'], 'L0_ffn_down_s': _L0_ffn_in['down_s'], 'L0_c': _L0_c, 'L0_wmod': _L0_wmod, 'L1_attn_wq': _L1_attn_in['wq'], 'L1_attn_bq': _L1_attn_in['bq'], 'L1_attn_wk': _L1_attn_in['wk'], 'L1_attn_bk': _L1_attn_in['bk'], 'L1_attn_wv': _L1_attn_in['wv'], 'L1_attn_bv': _L1_attn_in['bv'], 'L1_attn_wo': _L1_attn_in['wo'], 'L1_attn_bo': _L1_attn_in['bo'], 'L1_ffn_gate_w': _L1_ffn_in['gate_w'], 'L1_ffn_shared_wg': _L1_ffn_in['shared_wg'], 'L1_ffn_shared_wu': _L1_ffn_in['shared_wu'], 'L1_ffn_shared_wd': _L1_ffn_in['shared_wd'], 'L1_ffn_exp_wg': _L1_ffn_in['exp_wg'], 'L1_ffn_exp_wu': _L1_ffn_in['exp_wu'], 'L1_ffn_exp_wd': _L1_ffn_in['exp_wd'], 'L1_c': _L1_c, 'L1_wmod': _L1_wmod}
    _x0 = _d['L0_attn_x']
    _d['L0_attn_x'] = jax.random.normal(jax.random.fold_in(jax.random.key(seed), 1), (1, 2048, 256), dtype=_x0.dtype)
    del _x0
    return _d

def reference(L0_attn_x, L0_attn_q_w, L0_attn_q_b, L0_attn_k_w, L0_attn_k_b, L0_attn_v_w, L0_attn_v_b, L0_attn_o_w, L0_attn_o_b, L0_ffn_gate_w, L0_ffn_up_w, L0_ffn_down_w, L0_ffn_gate_s, L0_ffn_up_s, L0_ffn_down_s, L0_c, L0_wmod, L1_attn_wq, L1_attn_bq, L1_attn_wk, L1_attn_bk, L1_attn_wv, L1_attn_bv, L1_attn_wo, L1_attn_bo, L1_ffn_gate_w, L1_ffn_shared_wg, L1_ffn_shared_wu, L1_ffn_shared_wd, L1_ffn_exp_wg, L1_ffn_exp_wu, L1_ffn_exp_wd, L1_c, L1_wmod):

    def _L0_attn_ref(x, q_w, q_b, k_w, k_b, v_w, v_b, o_w, o_b):
        import jax, jax.numpy as jnp
        import numpy as np
        D_MODEL = 256
        NUM_HEADS = 16
        HEAD_DIM = D_MODEL // NUM_HEADS
        SCALE = HEAD_DIM ** (-0.5)
        ALPHA = 1.0
        B, T, D = x.shape
        H, HD = (NUM_HEADS, HEAD_DIM)

        def proj_split(w, bias):
            y = x @ w.T + bias
            return y.reshape(B, T, H, HD).transpose(0, 2, 1, 3).reshape(B * H, T, HD)
        Q = proj_split(q_w, q_b)
        K = proj_split(k_w, k_b)
        V = proj_split(v_w, v_b)
        S = jnp.einsum('hid,hjd->hij', K, Q) * SCALE
        idx = jnp.arange(T)
        delta = idx[:, None] - idx[None, :]
        decay = jnp.where(delta < 0, 0.0, -delta.astype(jnp.float32) ** ALPHA)
        S = jnp.where(delta < 0, -jnp.inf, S) + decay
        C = jax.nn.softmax(S, axis=-1)
        attn = jnp.einsum('hij,hjd->hid', C, V)
        attn = attn.reshape(B, H, T, HD).transpose(0, 2, 1, 3).reshape(B, T, D)
        return attn @ o_w.T + o_b

    def _L0_ffn_ref(x, gate_w, up_w, down_w, gate_s, up_s, down_s):
        import jax, jax.numpy as jnp
        import numpy as np
        HIDDEN = 256
        INTER = 704
        B, S = (2, 256)

        def _ternary(key, shape):
            return jax.random.randint(key, shape, -1, 2).astype(jnp.float32)
        b, s, h = x.shape
        xf = x.reshape(b * s, h)
        g = jnp.einsum('th,ih->ti', xf, gate_w) * gate_s
        u = jnp.einsum('th,ih->ti', xf, up_w) * up_s
        hdn = jax.nn.silu(g) * u
        out = jnp.einsum('ti,hi->th', hdn, down_w) * down_s
        return out.reshape(b, s, -1)

    def _L1_attn_ref(x, wq, bq, wk, bk, wv, bv, wo, bo):
        import jax, jax.numpy as jnp
        import numpy as np
        EMBED_DIM = 256
        NUM_HEADS = 16
        HEAD_DIM = EMBED_DIM // NUM_HEADS
        SCALE = EMBED_DIM ** (-0.5)
        b, t, d = x.shape
        h, hd = (NUM_HEADS, HEAD_DIM)
        q = (x @ wq + bq).reshape(b, t, h, hd).transpose(0, 2, 1, 3)
        k = (x @ wk + bk).reshape(b, t, h, hd).transpose(0, 2, 1, 3)
        v = (x @ wv + bv).reshape(b, t, h, hd).transpose(0, 2, 1, 3)
        scores = jnp.einsum('bhqd,bhkd->bhqk', q, k) * SCALE
        probs = jax.nn.softmax(scores, axis=-1)
        attn = jnp.einsum('bhqk,bhkd->bhqd', probs, v)
        attn = attn.transpose(0, 2, 1, 3).reshape(b, t, d)
        return attn @ wo + bo

    def _L1_ffn_ref(hidden_states, gate_w, shared_wg, shared_wu, shared_wd, exp_wg, exp_wu, exp_wd):
        import jax, jax.numpy as jnp
        import numpy as np
        HIDDEN = 256
        N_EXPERTS = 8
        N_SHARED = 2
        TOP_K = 2
        MOE_FF = 176
        SHARED_FF = N_SHARED * MOE_FF
        SCALE = 2.5
        BATCH, SEQ = (2, 128)
        B, S, D = hidden_states.shape
        T = B * S
        xf = hidden_states.reshape(T, D)
        scores = jax.nn.sigmoid(xf @ gate_w.T)
        topk_w, topk_idx = jax.lax.top_k(scores, TOP_K)
        topk_w = topk_w / (topk_w.sum(axis=-1, keepdims=True) + 1e-20)
        topk_w = topk_w * SCALE
        shared_out = jax.nn.silu(xf @ shared_wg.T) * (xf @ shared_wu.T) @ shared_wd.T
        h = jax.nn.silu(jnp.einsum('td,efd->etf', xf, exp_wg)) * jnp.einsum('td,efd->etf', xf, exp_wu)
        all_out = jnp.einsum('etf,edf->etd', h, exp_wd)
        picked = all_out[topk_idx, jnp.arange(T)[:, None]]
        routed_out = (topk_w[..., None] * picked).sum(axis=1)
        return (shared_out + routed_out).reshape(B, S, D)
    x = L0_attn_x
    mod = (_silu(L0_c) @ L0_wmod).reshape(L0_c.shape[0], 6, 1, -1)
    sa, ca, ga, sb, cb, gb = (mod[:, 0], mod[:, 1], mod[:, 2], mod[:, 3], mod[:, 4], mod[:, 5])
    ga = (2 * (ga >= 0) - 1) * jnp.maximum(jnp.abs(ga), 0.25)
    gb = (2 * (gb >= 0) - 1) * jnp.maximum(jnp.abs(gb), 0.25)
    h = _layernorm(x, axis=-1) * (1 + ca) + sa
    x = x + ga * _L0_attn_ref(h, L0_attn_q_w, L0_attn_q_b, L0_attn_k_w, L0_attn_k_b, L0_attn_v_w, L0_attn_v_b, L0_attn_o_w, L0_attn_o_b)
    h = _layernorm(x, axis=-1) * (1 + cb) + sb
    x = x + gb * _L0_ffn_ref(h, L0_ffn_gate_w, L0_ffn_up_w, L0_ffn_down_w, L0_ffn_gate_s, L0_ffn_up_s, L0_ffn_down_s)
    mod = (_silu(L1_c) @ L1_wmod).reshape(L1_c.shape[0], 6, 1, -1)
    sa, ca, ga, sb, cb, gb = (mod[:, 0], mod[:, 1], mod[:, 2], mod[:, 3], mod[:, 4], mod[:, 5])
    ga = (2 * (ga >= 0) - 1) * jnp.maximum(jnp.abs(ga), 0.25)
    gb = (2 * (gb >= 0) - 1) * jnp.maximum(jnp.abs(gb), 0.25)
    h = _layernorm(x, axis=-1) * (1 + ca) + sa
    x = x + ga * _L1_attn_ref(h, L1_attn_wq, L1_attn_bq, L1_attn_wk, L1_attn_bk, L1_attn_wv, L1_attn_bv, L1_attn_wo, L1_attn_bo)
    h = _layernorm(x, axis=-1) * (1 + cb) + sb
    x = x + gb * _L1_ffn_ref(h, L1_ffn_gate_w, L1_ffn_shared_wg, L1_ffn_shared_wu, L1_ffn_shared_wd, L1_ffn_exp_wg, L1_ffn_exp_wu, L1_ffn_exp_wd)
    return x

_drawn_inputs = setup_inputs


def setup_inputs(seed=0):
    import zlib

    import numpy as np

    out = dict(_drawn_inputs(seed))
    spreads = {'L1_attn_bq': (0.0, 0.8),
     'L1_attn_bk': (0.0, 0.8),
     'L1_attn_bv': (0.0, 0.504),
     'L1_attn_bo': (0.0, 0.334)}
    factors = {'L0_attn_q_w': 8.0,
     'L0_attn_q_b': 8.0,
     'L0_attn_k_w': 8.0,
     'L0_attn_k_b': 8.0,
     'L0_attn_v_w': 3.22,
     'L0_attn_v_b': 8.0,
     'L0_attn_o_w': 3.212,
     'L0_attn_o_b': 8.0,
     'L1_attn_wq': 8.0,
     'L1_attn_wk': 8.0,
     'L1_attn_wv': 8.0,
     'L1_attn_wo': 3.795,
     'L1_ffn_gate_w': 8.0,
     'L1_ffn_shared_wg': 8.0,
     'L1_ffn_shared_wu': 8.0,
     'L1_ffn_shared_wd': 8.0,
     'L1_ffn_exp_wg': 8.0,
     'L1_ffn_exp_wu': 8.0,
     'L1_ffn_exp_wd': 8.0}
    for name, (base, spread) in spreads.items():
        noise = np.random.default_rng([zlib.crc32(name.encode()), seed]).standard_normal(out[name].shape)
        drawn = base * np.exp(spread * noise) if base else spread * noise
        out[name] = jnp.asarray(drawn.astype(out[name].dtype))
    for name, factor in factors.items():
        out[name] = (out[name] * factor).astype(out[name].dtype)
    return out
```

```python
from contextlib import ExitStack

import numpy as np
import concourse.bass as bass
from concourse import mybir

F32 = mybir.dt.float32
BF16 = mybir.dt.bfloat16
ALU = mybir.AluOpType
ACT = mybir.ActivationFunctionType
AX = mybir.AxisListType

P = 128
T = 2048
D = 256
KD = D // P
NT = T // P
CH = 512
NCH = T // CH
TPC = CH // P
H = 16
HD = D // H
HG = 4
NG = H // HG
GF = HG * HD
VW = HD + 1
SLOTS_ROW = (0, 0, 1, 1, 0, 2)
SLOTS_COL = (0, 1, 0, 1, 2, 0)
CR = 6
KS = CR + HD * len(SLOTS_ROW)
SCALES = (HD ** -0.5, D ** -0.5)
ROUND = 12582912.0
EPS = 1e-5
NE = 8
FE = 176
F0 = 704
F1 = NE * FE + 2 * FE
FS = (F0, F1)
NC = tuple(-(-f // P) for f in FS)
RC = NE * FE // P
CAUSAL = (True, False)
NLAY = 2


def fsize(layer, c):
    return min(P, FS[layer] - P * c)


def steps_of(layer, n):
    return TPC * (n // NG + 1) if CAUSAL[layer] else NT


def plan(layer):
    units = NCH * NG
    blocks, ends = [], []
    for n in range(units):
        chunks = n // NG + 1 if CAUSAL[layer] else NCH
        blocks += [(n, h, r, q) for h in range(HG) for r in range(TPC) for q in range(chunks)]
        ends.append(len(blocks))
    start = [sum(steps_of(layer, m) for m in range(n)) for n in range(units)]
    total = start[-1] + steps_of(layer, units - 1)
    slots, done = [], ends[0]
    first = blocks[:done]
    for s in range(-1, total):
        want = len(blocks)
        for n in range(1, units):
            a, b = start[n - 1] - 4, start[n] - 4
            if a <= s < b:
                want = ends[n - 1] + (ends[n] - ends[n - 1]) * (s - a) // (b - a)
        want = max(want, done)
        slots.append(blocks[done:want])
        done = want
    return first, slots, start, total


def adaln_two_layers(nc, a):
    ctx = ExitStack()
    with ctx:
        def sb(name, shape, dt=F32):
            return ctx.enter_context(nc.sbuf_tensor(name, shape, dt))

        def sem(name):
            return ctx.enter_context(nc.semaphore(name))

        x_sb = sb("x_sb", [P, NT, D])
        key_region = sb("key_region", [P, H * T // 2])
        v_region = sb("v_region", [P, NT * H * VW])
        row_region = sb("row_region", [P, NG * HG * CH // 2])
        prob_region = sb("prob_region", [P, 3 * HG * CH])
        attn_region = sb("attn_region", [P, NG * CH])
        ffn_w = sb("ffn_w", [P, 2, KD * F1])
        w_row = sb("w_row", [P, KD, D])
        w_col = sb("w_col", [P, KD, D])
        w_v = sb("w_v", [P, KD, D])
        w_o = sb("w_o", [P, NG, D])
        b_row = sb("b_row", [P, KD])
        b_col = sb("b_col", [P, KD])
        b_colr = sb("b_colr", [P, KD])
        b_v = sb("b_v", [P, D])
        b_o = sb("b_o", [P, D])
        out_sb = sb("out_sb", [P, CH])
        den = sb("den", [P, CH])
        mrow_t = sb("mrow_t", [P, CH], BF16)
        mpart = sb("mpart", [P, HG * TPC, NCH])
        mx = sb("mx", [P, HG * TPC])
        mp = sb("mp", [P, HG * TPC, 32], BF16)
        ident = sb("ident", [P, P])
        identb = sb("identb", [P, P], BF16)
        neg_m = sb("neg_m", [P, P], BF16)
        neg_e = sb("neg_e", [P, P], BF16)
        gab = sb("gab", [P, NLAY, 2 * D])
        modc = sb("modc", [P, NLAY, 8])
        stats = sb("stats", [P, TPC, 6])
        mv = sb("mv", [P, 2, TPC, 2])
        rstd = sb("rstd", [P, 2, TPC])
        vare = sb("vare", [P, TPC])
        half = sb("half", [P, TPC])
        c_sb = sb("c_sb", [P, 2 * KD])
        ce = sb("ce", [P, 2 * KD])
        cs = sb("cs", [P, 2 * KD])
        gate_s = sb("gate_s", [P, NC[0]])
        up_s = sb("up_s", [P, NC[0]])
        down_s = sb("down_s", [P, D])
        gate_w = sb("gate_w", [P, KD, NE])
        tri = sb("tri", [P, NE, NE])
        esel = sb("esel", [3 * NE, RC, P], BF16)

        keys = key_region[:, :].bitcast(BF16).rearrange("p (h t) -> p h t", h=H)
        v_sb = v_region[:, :].rearrange("p (t h c) -> p t h c", t=NT, h=H)
        rows = row_region[:, :].bitcast(BF16).rearrange("p (g h t) -> p g h t", g=NG, h=HG)
        probs = prob_region[:, :].rearrange("p (b h t) -> p b h t", b=3, h=HG)
        attn_t = attn_region[:, :].rearrange("p (g t) -> p g t", g=NG)
        wmod = key_region[:, 0:KD * 6 * D * NLAY].rearrange("p (l k n) -> p l k n", l=NLAY, k=KD)
        o1 = KD * 6 * D * NLAY
        csb = key_region[:, o1:o1 + 2 * KD * P].rearrange("p (k n) -> p k n", k=2 * KD)
        o1 += 2 * KD * P
        gtmp = key_region[:, o1:o1 + 3 * 2 * D].rearrange("p (k n) -> p k n", k=3)
        hT = prob_region[:, 0:KD * T].rearrange("p (k t) -> p k t", k=KD)
        SW = CH * 2 + 3 * CH // 2
        stage = [key_region[:, b * SW:(b + 1) * SW] for b in range(3)]
        st_f = [s[:, 0:CH] for s in stage]
        st_r = [s[:, CH:2 * CH] for s in stage]
        st_p = [s[:, 2 * CH:SW].bitcast(BF16).rearrange("p (k t) -> p k t", k=3) for s in stage]
        xh = attn_region[:, :].rearrange("p (b t d) -> p b t d", b=2, t=TPC)
        HW = NC[1] * CH
        hid = [key_region[:, b * HW:(b + 1) * HW].rearrange("p (c t) -> p c t", c=NC[1]) for b in range(2)]
        sil = [key_region[:, 2 * HW + b * CH:2 * HW + (b + 1) * CH] for b in range(2)]
        utmp = [key_region[:, 2 * HW + (2 + b) * CH:2 * HW + (3 + b) * CH] for b in range(2)]
        down = v_region[:, 0:NC[1] * D].rearrange("p (c d) -> p c d", c=NC[1])
        up_gate = [[ffn_w[:, i, 0:KD * FS[y]].rearrange("p (k f) -> p k f", k=KD) for i in range(2)]
                   for y in range(NLAY)]
        ro = [0]

        def take(n):
            ro[0] += n
            return row_region[:, ro[0] - n:ro[0]]

        r_s = take(NT * NE).rearrange("p (t e) -> p t e", t=NT)
        r_gt = take(NT * NE * NE).rearrange("p (t e f) -> p t e f", t=NT, e=NE)
        r_eq = take(NT * NE * NE).rearrange("p (t e f) -> p t e f", t=NT, e=NE)
        r_rank = take(NT * NE).rearrange("p (t e) -> p t e", t=NT)
        r_w = take(NT * NE).rearrange("p (t e) -> p t e", t=NT)
        r_sum = take(NT)
        r_inv = take(NT)
        r_lo = take(NT * NE).rearrange("p (t e) -> p t e", t=NT)
        r_p = take(NT * 3 * NE // 2).bitcast(BF16).rearrange("p (t k e) -> p t k e", t=NT, k=3)
        wT = take(T // 2).bitcast(BF16)

        psum = ctx.enter_context(nc.psum_tensor("psum", [P, 8, CH], F32))

        def bank(b):
            return psum[:, b, :]

        parts = nc.dram_tensor("parts", (2, 3, D, T), BF16, kind="Internal").ap()

        s_x = sem("x_loaded")
        s_const = sem("constants_loaded")
        s_wmod = sem("modulation_inputs_loaded")
        s_wattn = sem("attention_weights_loaded")
        s_wffn = sem("ffn_weights_loaded")
        s_wdown = sem("down_weights_loaded")
        s_dve = sem("vector_chain")
        s_act = sem("scalar_chain")
        s_pool = sem("gpsimd_chain")
        s_ce = sem("exp_c_done")
        s_cs = sem("silu_c_spread")
        s_modp = sem("modulation_product")
        s_mod = sem("modulation_ready")
        s_wo = sem("output_weights_scaled")
        s_wd = sem("down_weights_scaled")
        s_obg = sem("output_bias_added")
        s_mv = sem("ln_stats_ready")
        s_rstd = sem("ln_rstd_ready")
        s_xh = sem("normed_ready")
        s_tr = sem("normed_transposed")
        s_hte = sem("h_ready")
        s_pj = sem("projection_product")
        s_qf = sem("projection_evacuated")
        s_bs = sem("column_bias_scaled")
        s_h = sem("high_part_ready")
        s_l = sem("low_part_ready")
        s_split = [sem(f"parts_stored{b}") for b in range(3)]
        s_vp = sem("value_product")
        s_ve = sem("values_ready")
        s_key = [sem(f"keys_loaded{g}") for g in range(NG)]
        s_row = [sem(f"rows_loaded{g}") for g in range(NG)]
        s_mb = sem("max_block_product")
        s_mr = sem("max_block_reduced")
        s_mp = sem("max_parts_ready")
        s_mt = sem("max_transposed")
        s_mtc = sem("max_rows_copied")
        s_mrow = sem("max_rows_placed")
        s_e = sem("scores_ready")
        s_p = sem("probs_ready")
        s_pv = sem("probs_used")
        s_oc = sem("attn_copied")
        s_on = sem("attn_normalised")
        s_op = sem("output_product")
        s_xa = sem("attn_added")
        s_g = sem("gate_product")
        s_u = sem("up_product")
        s_sil = sem("silu_ready")
        s_hid = sem("hidden_ready")
        s_dn = sem("down_product")
        s_xd = sem("ffn_added")
        s_lg = sem("router_product")
        s_le = sem("router_exp")
        s_rp = sem("router_parts_ready")
        s_rt = sem("router_transposed")
        s_wt = sem("router_rows_ready")
        s_out = sem("output_stored")

        plans = [plan(y) for y in range(NLAY)]
        STEPS = [p[3] for p in plans]
        S0 = [0, STEPS[0], STEPS[0] + STEPS[1]]
        MB = [sum(len(s) for s in p[1]) + len(p[0]) for p in plans]
        M0 = [0, MB[0], MB[0] + MB[1]]
        NU = NCH * NG
        K0 = [0, NC[0] * NCH, (NC[0] + NC[1]) * NCH]

        def slot_walk(y):
            first, slots, start, total = plans[y]
            for s in range(-1, total):
                n = max(m for m in range(NU) if start[m] <= max(s, 0))
                yield s, n, s - start[n], slots[s + 1]

        def unit_steps(y, n):
            return S0[y] + plans[y][2][n] + steps_of(y, n)

        def mt_slot(y, n, k):
            return n + 1 if n + 1 < NU and k == steps_of(y, n) - 3 else None

        def oproj_slot(n, k):
            return (n // NG - 1, k - 4) if n % NG == 0 and n > 0 and k in (4, 5) else None

        def ffn_walk(y):
            for tc in range(NCH):
                for c in range(NC[y]):
                    yield "hid", tc, c
                    if c == 1 and tc > 0:
                        yield "down", tc - 1, 0
            yield "down", NCH - 1, 0

        block = ctx.enter_context(nc.Block())

        @block.sync
        def _(sp):
            def load_attn(y):
                for dst, name in ((w_row, "w_row"), (w_col, "w_col"), (w_v, "w_v")):
                    sp.dma_start(dst[:, :, :], a[f"{name}{y}"].rearrange("(k p) n -> p k n", p=P)).then_inc(s_wattn, 16)
                sp.dma_start(w_o[:, :, :], a[f"w_o{y}"].rearrange("(k p) n -> p k n", p=P)).then_inc(s_wattn, 16)
                sp.dma_start(b_row[:, :], a[f"b_row{y}"]).then_inc(s_wattn, 16)
                sp.dma_start(b_colr[:, :], a[f"b_col{y}"]).then_inc(s_wattn, 16)
                sp.dma_start(b_v[:, :], a[f"b_v{y}"].partition_broadcast(P)).then_inc(s_wattn, 16)
                sp.dma_start(b_o[:, :], a[f"b_o{y}"].partition_broadcast(P)).then_inc(s_wattn, 16)

            def load_ffn(y):
                for i, name in enumerate(("w_gate", "w_up")):
                    sp.dma_start(up_gate[y][i], a[f"{name}{y}"].rearrange("(k p) n -> p k n", p=P)).then_inc(s_wffn, 16)

            def load_down(y):
                full = FS[y] // P
                sp.dma_start(down[:, 0:full, :], a[f"w_down{y}"][0:full * P, :].rearrange("(c p) d -> p c d", p=P)).then_inc(s_wdown, 16)
                sp.dma_start(down[0:FS[y] - full * P, full, :], a[f"w_down{y}"][full * P:FS[y], :]).then_inc(s_wdown, 16)

            def load_rows(y, n):
                i, g = n // NG, n % NG
                if n >= NG:
                    sp.wait_ge(s_e, 2 * unit_steps(y, n - NG))
                sp.dma_start(rows[0:CR, g, :, :], a[f"row_const{y}"][:, :, i * CH:(i + 1) * CH]).then_inc(s_row[g], 16)
                for k, part in enumerate(SLOTS_ROW):
                    src = parts[0, part, g * GF:(g + 1) * GF, i * CH:(i + 1) * CH].rearrange("(h c) t -> c h t", c=HD)
                    sp.dma_start(rows[CR + HD * k:CR + HD * (k + 1), g, :, :], src).then_inc(s_row[g], 16)

            def load_keys(g):
                sp.dma_start(keys[0:CR, g * HG:(g + 1) * HG, :], a["col_const"]).then_inc(s_key[g], 16)
                for k, part in enumerate(SLOTS_COL):
                    src = parts[1, part, g * GF:(g + 1) * GF, :].rearrange("(h c) t -> c h t", c=HD)
                    sp.dma_start(keys[CR + HD * k:CR + HD * (k + 1), g * HG:(g + 1) * HG, :], src).then_inc(s_key[g], 16)

            sp.dma_start(c_sb[:, :], a["c"]).then_inc(s_wmod, 16)
            for tc in range(NCH):
                sp.dma_start(x_sb[:, tc * TPC:(tc + 1) * TPC, :],
                             a["x"][tc * CH:(tc + 1) * CH, :].rearrange("(t p) d -> p t d", p=P)).then_inc(s_x, 16)
            for y in range(NLAY):
                sp.dma_start(wmod[:, y, :, :], a[f"wmod{y}"].rearrange("(k p) n -> p k n", p=P)).then_inc(s_wmod, 16)
            load_attn(0)
            for dst, name in ((ident, "ident"), (identb, "identb"), (neg_m, "neg_m"), (neg_e, "neg_e"),
                              (gate_s, "gate_s"), (up_s, "up_s")):
                sp.dma_start(dst[:, :], a[name]).then_inc(s_const, 16)
            sp.dma_start(down_s[:, :], a["down_s"].partition_broadcast(P)).then_inc(s_const, 16)
            sp.dma_start(gate_w[:, :, :], a["gate_w"].rearrange("(k p) n -> p k n", p=P)).then_inc(s_const, 16)
            sp.dma_start(tri[:, :, :], a["tri"].partition_broadcast(P)).then_inc(s_const, 16)
            sp.dma_start(esel[:, :, :], a["esel"]).then_inc(s_const, 16)
            load_ffn(0)
            for y in range(NLAY):
                for tc in range(NCH):
                    for side in range(2):
                        for f in range(KD):
                            k = (y * NCH + tc) * 4 + side * KD + f
                            sp.wait_ge(s_l, k + 1)
                            sp.dma_start(parts[side, :, f * P:(f + 1) * P, tc * CH:(tc + 1) * CH].rearrange("k f t -> f k t"),
                                         st_p[k % 3]).then_inc(s_split[k % 3], 16)
                for b in range(3):
                    jobs = len([k for k in range(16 * (y + 1)) if k % 3 == b])
                    sp.wait_ge(s_split[b], 16 * jobs)
                for g in range(NG):
                    load_rows(y, g)
                    load_keys(g)
                for s, n, k, _blocks in slot_walk(y):
                    if k == 0 and n > 0:
                        if n + 3 < NU:
                            load_rows(y, n + 3)
                    m = 0 if s == -1 else mt_slot(y, n, k)
                    if m is not None:
                        sp.wait_ge(s_mtc, y * NU + m + 1)
                        for h in range(HG):
                            sp.dma_start(rows[0:2, m % NG, h, :], mrow_t[32 * h:32 * h + 2, :]).then_inc(s_mrow, 16)
                sp.wait_ge(s_pv, S0[y + 1])
                load_down(y)
                if y == 0:
                    sp.wait_ge(s_op, 8)
                    load_attn(1)
                    sp.wait_ge(s_u, K0[1])
                    load_ffn(1)
            for t in range(NT):
                sp.wait_ge(s_xd, NT + t + 1)
                sp.dma_start(a["out"][t * P:(t + 1) * P, :], x_sb[:, t, :]).then_inc(s_out, 16)
            sp.wait_ge(s_out, 16 * NT)

        @block.gpsimd
        def _(pool):
            chain = [0]

            def link(ins):
                chain[0] += 1
                ins.then_inc(s_pool, 1)
                pool.wait_ge(s_pool, chain[0])

            def ln(q):
                for tc in range(NCH):
                    j = q * NCH + tc
                    pool.wait_ge(s_mv, j + 1)
                    link(nc.gpsimd.tensor_scalar(vare[:, :], mv[:, tc % 2, :, 1], EPS, None, ALU.add))
                    if j >= 2:
                        pool.wait_ge(s_xh, j - 1)
                    nc.gpsimd.tensor_tensor(rstd[:, tc % 2, :], vare[:, :], half[:, :], ALU.pow).then_inc(s_rstd, 1)
                    if tc + 1 < NCH:
                        pool.wait_ge(s_rstd, j + 1)

            def scale_wo(y):
                pool.wait_ge(s_mod, y + 1)
                pool.wait_ge(s_wattn, 128 * (y + 1))
                for g in range(NG):
                    link(nc.gpsimd.tensor_tensor(w_o[:, g, :], w_o[:, g, :], gab[:, y, 0:D], ALU.mult))
                nc.gpsimd.tensor_tensor(b_o[:, :], b_o[:, :], gab[:, y, 0:D], ALU.mult).then_inc(s_wo, 1)
                pool.wait_ge(s_wo, y + 1)

            def add_bias(y):
                pool.wait_ge(s_xh, (2 * y + 1) * NCH)
                for t in range(NT):
                    ins = nc.gpsimd.tensor_tensor(x_sb[:, t, :], x_sb[:, t, :], b_o[:, :], ALU.add)
                ins.then_inc(s_obg, 1)

            def scale_down(y):
                pool.wait_ge(s_wdown, 32 * (y + 1))
                for c in range(NC[y]):
                    f = fsize(y, c)
                    ins = nc.gpsimd.tensor_tensor(down[0:f, c, :], down[0:f, c, :], gab[0:f, y, D:2 * D], ALU.mult)
                ins.then_inc(s_wd, 1)

            link(nc.gpsimd.memset(half[:, :], -0.5))
            for y in range(NLAY):
                ln(2 * y)
                scale_wo(y)
                add_bias(y)
                ln(2 * y + 1)
                scale_down(y)

        @block.tensor
        def _(pe):
            pe.wait_ge(s_cs, 1)
            pe.wait_ge(s_wmod, 48)
            for y in range(NLAY):
                for i, col in enumerate((2, 5)):
                    for k in range(KD):
                        mm = pe.matmul(bank(2 * y)[:, i * D:(i + 1) * D], csb[:, y * KD + k, :],
                                       wmod[:, y, k, col * D:(col + 1) * D], start=(k == 0), stop=(k == KD - 1))
                for i in range(8):
                    col = (0, 1, 3, 4)[i // 2] * D + (i % 2) * P
                    for k in range(KD):
                        mm = pe.matmul(bank(2 * y + 1)[:, i:i + 1], wmod[:, y, k, col:col + P],
                                       cs[:, y * KD + k:y * KD + k + 1], start=(k == 0), stop=(k == KD - 1))
                mm.then_inc(s_modp, 1)
            pe.wait_ge(s_const, 160)

            def ln(q):
                for tc in range(NCH):
                    j = q * NCH + tc
                    pe.wait_ge(s_xh, j + 1)
                    for c in range(KD):
                        if j == 0:
                            pe.wait_ge(s_mod, 1)
                        else:
                            pe.wait_ge(s_hte, 2 * (j - 1) + c + 1)
                        for t in range(TPC):
                            mm = pe.transpose(bank(c)[:, t * P:(t + 1) * P], xh[:, tc % 2, t, c * P:(c + 1) * P], ident[:, :])
                        mm.then_inc(s_tr, 1)

            def qkv(y):
                pe.wait_ge(s_wattn, 128 * (y + 1))
                pe.wait_ge(s_mod, NLAY)
                for tc in range(NCH):
                    pe.wait_ge(s_hte, 16 * y + 2 * (tc + 1))
                    tok = slice(tc * CH, (tc + 1) * CH)
                    for side, w in enumerate((w_row, w_col)):
                        for f in range(KD):
                            j = (y * NCH + tc) * 4 + side * KD + f
                            if j >= 2:
                                pe.wait_ge(s_qf, j - 1)
                            for k in range(KD):
                                mm = pe.matmul(bank(2 + j % 2), w[:, k, f * P:(f + 1) * P], hT[:, k, tok],
                                               start=(k == 0), stop=(k == KD - 1))
                            mm.then_inc(s_pj, 1)
                for t in range(NT):
                    v = y * NT + t
                    if v >= 2:
                        pe.wait_ge(s_ve, v - 1)
                    for k in range(KD):
                        mm = pe.matmul(bank(4 + v % 2)[:, 0:D], hT[:, k, t * P:(t + 1) * P], w_v[:, k, :],
                                       start=(k == 0), stop=(k == KD - 1))
                    mm.then_inc(s_vp, 1)

            def attention(y):
                mb = [M0[y]]

                def max_block(n, h, r, q):
                    i, g = n // NG, n % NG
                    b = mb[0]
                    mb[0] += 1
                    if (h, r, q) == (0, 0, 0):
                        pe.wait_ge(s_row[g], 112 * (y * NCH + i + 1))
                        pe.wait_ge(s_key[g], 112 * (y + 1))
                    if b >= 2:
                        pe.wait_ge(s_mr, b - 1)
                    last = CAUSAL[y] and q == i
                    w = (r + 1) * P if last else CH
                    out = bank(4 + b % 2)
                    mm = pe.matmul(out[:, 0:w], rows[0:KS, g, h, r * P:(r + 1) * P],
                                   keys[0:KS, g * HG + h, q * CH:q * CH + w], start=True, stop=not last)
                    if last:
                        mm = pe.matmul(out[:, w - P:w], identb[:, :], neg_m[:, :], start=False, stop=True)
                    mm.then_inc(s_mb, 1)

                def max_transpose(n):
                    u = y * NU + n
                    pe.wait_ge(s_mp, u + 1)
                    if n % NG == 1 and n > 1:
                        pe.wait_ge(s_xa, 8 * y + 2 * (n // NG))
                    elif n >= 2:
                        pe.wait_ge(s_oc, u - 1)
                    for h in range(HG):
                        for r in range(TPC):
                            mm = pe.matmul(psum[32 * h:32 * h + 32, 6 + n % 2, r * P:(r + 1) * P],
                                           mp[:, h * TPC + r, :], identb[:, :], start=True, stop=True)
                    mm.then_inc(s_mt, 1)

                def scores(s, n, jt, pair):
                    i, g = n // NG, n % NG
                    e = 2 * (S0[y] + s) + pair
                    if jt == 0 and pair == 0:
                        pe.wait_ge(s_mrow, 64 * (y * NU + n + 1))
                    if e >= 2:
                        pe.wait_ge(s_p, e - 1)
                    off = max(0, jt - TPC * i) * P if CAUSAL[y] else 0
                    diag = CAUSAL[y] and jt >= TPC * i
                    for hh in range(2):
                        h = 2 * pair + hh
                        out = bank(2 * (e % 2) + hh)
                        mm = pe.matmul(out[:, off:CH], keys[0:KS, g * HG + h, jt * P:(jt + 1) * P],
                                       rows[0:KS, g, h, off:CH], start=True, stop=not diag)
                        if diag:
                            mm = pe.matmul(out[:, off:off + P], identb[:, :], neg_e[:, :], start=False, stop=True)
                    mm.then_inc(s_e, 1)

                def values(s, n, jt):
                    i, g = n // NG, n % NG
                    pe.wait_ge(s_p, 2 * (S0[y] + s + 1))
                    if jt == 0:
                        pe.wait_ge(s_mtc, y * NU + n + 1)
                    off = max(0, jt - TPC * i) * P if CAUSAL[y] else 0
                    for h in range(HG):
                        mm = pe.matmul(psum[32 * h:32 * h + VW, 6 + n % 2, off:CH], v_sb[:, jt, g * HG + h, :],
                                       probs[:, (S0[y] + s) % 3, h, off:CH], start=(jt == 0), stop=(jt == steps_of(y, n) - 1))
                    mm.then_inc(s_pv, 1)

                def output(i, half_):
                    if half_ == 0:
                        pe.wait_ge(s_on, y * NU + NG * (i + 1))
                        pe.wait_ge(s_wo, y + 1)
                    else:
                        pe.wait_ge(s_xa, 8 * y + 2 * i + 1)
                    for r in range(2):
                        t = 2 * half_ + r
                        for g in range(NG):
                            mm = pe.matmul(bank(7)[:, r * D:(r + 1) * D], attn_t[:, g, t * P:(t + 1) * P], w_o[:, g, :],
                                           start=(g == 0), stop=(g == NG - 1))
                    mm.then_inc(s_op, 1)

                pe.wait_ge(s_qf, 16 * (y + 1))
                pe.wait_ge(s_ve, NT * (y + 1))
                first = plans[y][0]
                for b in first:
                    max_block(*b)
                before = None
                for s, n, k, blocks in slot_walk(y):
                    if s == -1:
                        max_transpose(0)
                    else:
                        if oproj_slot(n, k):
                            output(*oproj_slot(n, k))
                        if mt_slot(y, n, k) is not None:
                            max_transpose(mt_slot(y, n, k))
                    quarter = [len(blocks) * m // 4 for m in range(5)]
                    for m in range(4):
                        for b in blocks[quarter[m]:quarter[m + 1]]:
                            max_block(*b)
                        if m < 2 and s >= 0:
                            scores(s, n, k, m)
                        if m == 2 and before:
                            values(*before)
                    before = (s, n, k) if s >= 0 else None
                values(*before)
                output(NCH - 1, 0)
                output(NCH - 1, 1)

            def router():
                for t in range(NT):
                    if t == 0:
                        pe.wait_ge(s_hte, 32)
                    for k in range(KD):
                        mm = pe.matmul(bank(7)[:, t * NE:(t + 1) * NE], hT[:, k, t * P:(t + 1) * P], gate_w[:, k, :],
                                       start=(k == 0), stop=(k == KD - 1))
                mm.then_inc(s_lg, 1)
                pe.wait_ge(s_rp, 1)
                for tc in range(NCH):
                    if tc >= 2:
                        pe.wait_ge(s_wt, tc - 1)
                    for r in range(TPC):
                        t = tc * TPC + r
                        mm = pe.matmul(psum[0:3 * NE, 4 + tc % 2, r * P:(r + 1) * P],
                                       r_p[:, t, :, :].rearrange("p k e -> p (k e)"), identb[:, :], start=True, stop=True)
                    mm.then_inc(s_rt, 1)
                pe.wait_ge(s_wt, NCH)

            def ffn(y):
                pe.wait_ge(s_wffn, 32 * (y + 1))
                pe.wait_ge(s_xa, 8 * (y + 1))
                pe.wait_ge(s_mr, M0[y + 1])
                if y == 1:
                    router()
                for what, tc, c in ffn_walk(y):
                    tok = slice(tc * CH, (tc + 1) * CH)
                    if what == "hid":
                        k = K0[y] + tc * NC[y] + c
                        f = fsize(y, c)
                        pe.wait_ge(s_hte, 16 * y + 8 + 2 * (tc + 1))
                        if c < 2 and tc == 0:
                            pe.wait_ge(s_hte, 16 * y + 16)
                        if k >= 2:
                            pe.wait_ge(s_sil, k - 1)
                        for d in range(KD):
                            mm = pe.matmul(psum[0:f, k % 2, :], up_gate[y][0][:, d, c * P:c * P + f], hT[:, d, tok],
                                           start=(d == 0), stop=(d == KD - 1))
                        mm.then_inc(s_g, 1)
                        if k >= 2:
                            pe.wait_ge(s_hid, k - 1)
                        for d in range(KD):
                            mm = pe.matmul(psum[0:f, 2 + k % 2, :], up_gate[y][1][:, d, c * P:c * P + f], hT[:, d, tok],
                                           start=(d == 0), stop=(d == KD - 1))
                        if y == 1 and c < RC:
                            mm = pe.matmul(bank(4 + k % 2), esel[:, c, :], wT[0:3 * NE, tok], start=True, stop=True)
                        mm.then_inc(s_u, 1)
                    else:
                        pe.wait_ge(s_hid, K0[y] + (tc + 1) * NC[y])
                        pe.wait_ge(s_wd, y + 1)
                        for r in range(TPC):
                            j = y * NT + tc * TPC + r
                            if j >= 2:
                                pe.wait_ge(s_xd, j - 1)
                            for cc in range(NC[y]):
                                f = fsize(y, cc)
                                mm = pe.matmul(bank(6 + j % 2)[:, 0:D], hid[tc % 2][0:f, cc, r * P:(r + 1) * P],
                                               down[0:f, cc, :], start=(cc == 0), stop=(cc == NC[y] - 1))
                            mm.then_inc(s_dn, 1)

            for y in range(NLAY):
                if y == 1:
                    pe.wait_ge(s_sil, K0[1])
                    pe.wait_ge(s_hid, K0[1])
                    pe.wait_ge(s_xd, NT)
                ln(2 * y)
                qkv(y)
                attention(y)
                pe.wait_ge(s_p, 2 * S0[y + 1])
                ln(2 * y + 1)
                ffn(y)

        @block.scalar
        def _(act):
            chain = [0]

            def link(ins):
                chain[0] += 1
                ins.then_inc(s_act, 1)
                act.wait_ge(s_act, chain[0])

            act.wait_ge(s_wmod, 48)
            nc.scalar.activation(ce[:, :], c_sb[:, :], ACT.Exp, scale=-1.0).then_inc(s_ce, 1)
            act.wait_ge(s_mod, NLAY)

            def ln(q):
                y = q // 2
                if q == 1 or q == 3:
                    act.wait_ge(s_pv, S0[y + 1])
                if q == 2:
                    act.wait_ge(s_u, K0[1])
                for tc in range(NCH):
                    for c in range(KD):
                        act.wait_ge(s_tr, 2 * (q * NCH + tc) + c + 1)
                        i = 4 * (q % 2) + c
                        nc.scalar.activation(hT[:, c, tc * CH:(tc + 1) * CH], bank(c), ACT.Identity,
                                             bias=modc[:, y, i:i + 1], scale=modc[:, y, i + 2:i + 3]).then_inc(s_hte, 1)

            def qkv(y):
                if y == 1:
                    act.wait_ge(s_dn, NT)
                for tc in range(NCH):
                    for side in range(2):
                        for f in range(KD):
                            k = (y * NCH + tc) * 4 + side * KD + f
                            b = k % 3
                            act.wait_ge(s_pj, k + 1)
                            if k >= 3:
                                act.wait_ge(s_l, k - 2)
                                act.wait_ge(s_split[b], 16 * (k // 3))
                            act.wait_ge(s_bs, y + 1)
                            nc.scalar.activation(st_f[b], bank(2 + k % 2), ACT.Identity,
                                                 bias=(b_row, b_col)[side][:, f:f + 1],
                                                 scale=(1.0, SCALES[y])[side]).then_inc(s_qf, 1)
                            act.wait_ge(s_qf, k + 1)
                            nc.scalar.activation(st_p[b][:, 0, :], st_f[b], ACT.Identity).then_inc(s_h, 1)

            def attention(y):
                act.wait_ge(s_vp, NT * (y + 1))
                for s, n, k, _blocks in slot_walk(y):
                    if s >= 0:
                        i = n // NG
                        off = max(0, k - TPC * i) * P if CAUSAL[y] else 0
                        for pair in range(2):
                            e = 2 * (S0[y] + s) + pair
                            act.wait_ge(s_e, e + 1)
                            if S0[y] + s >= 3:
                                act.wait_ge(s_pv, S0[y] + s - 2)
                            nc.scalar.activation(probs[:, (S0[y] + s) % 3, 2 * pair:2 * pair + 2, off:CH],
                                                 psum[:, 2 * (e % 2):2 * (e % 2) + 2, off:CH], ACT.Exp).then_inc(s_p, 1)
                        if k == 0 and n > 0:
                            copy_out(y, n - 1)
                    m = 0 if s == -1 else mt_slot(y, n, k)
                    if m is not None:
                        act.wait_ge(s_mt, y * NU + m + 1)
                        act.wait_ge(s_mrow, 64 * (y * NU + m)) if y * NU + m else None
                        nc.scalar.activation(mrow_t[:, :], bank(6 + m % 2), ACT.Identity).then_inc(s_mtc, 1)
                copy_out(y, NU - 1)

            def copy_out(y, n):
                u = y * NU + n
                act.wait_ge(s_pv, unit_steps(y, n))
                if u:
                    act.wait_ge(s_on, u)
                nc.scalar.activation(out_sb[:, :], bank(6 + n % 2), ACT.Identity).then_inc(s_oc, 1)

            def ffn(y):
                if y == 1:
                    act.wait_ge(s_lg, 1)
                    nc.scalar.activation(r_s[:, :, :], bank(7)[:, 0:NT * NE].rearrange("p (t e) -> p t e", t=NT),
                                         ACT.Exp, scale=-1.0).then_inc(s_le, 1)
                for what, tc, c in ffn_walk(y):
                    if what == "hid":
                        k = K0[y] + tc * NC[y] + c
                        f = fsize(y, c)
                        act.wait_ge(s_g, k + 1)
                        if k >= 2:
                            act.wait_ge(s_hid, k - 1)
                        nc.scalar.activation(sil[k % 2][0:f, :], psum[0:f, k % 2, :], ACT.Silu,
                                             scale=gate_s[0:f, c:c + 1] if y == 0 else 1.0).then_inc(s_sil, 1)

            for y in range(NLAY):
                ln(2 * y)
                qkv(y)
                attention(y)
                ln(2 * y + 1)
                ffn(y)

        @block.vector
        def _(dve):
            chain = [0]

            def link(ins):
                chain[0] += 1
                ins.then_inc(s_dve, 1)
                dve.wait_ge(s_dve, chain[0])

            V = nc.vector
            link(V.memset(mp[:, :, :], 0.0))
            dve.wait_ge(s_ce, 1)
            link(V.tensor_scalar(ce[:, :], ce[:, :], 1.0, None, ALU.add))
            link(V.reciprocal(ce[:, :], ce[:, :]))
            link(V.tensor_tensor(cs[:, :], ce[:, :], c_sb[:, :], ALU.mult))
            for k in range(2 * KD):
                ins = V.tensor_copy(csb[:, k, :], cs[:, k:k + 1].to_broadcast([P, P]))
            ins.then_inc(s_cs, 1)
            for y in range(NLAY):
                dve.wait_ge(s_modp, y + 1)
                g = gab[:, y, :]
                link(V.tensor_copy(g, bank(2 * y)))
                link(V.tensor_copy(modc[:, y, :], bank(2 * y + 1)[:, 0:8]))
                for i in (2, 6):
                    link(V.tensor_scalar(modc[:, y, i:i + 2], modc[:, y, i:i + 2], 1.0, None, ALU.add))
                link(V.tensor_scalar(gtmp[:, 0, :], g, 0.0, 2.0, ALU.is_ge, ALU.mult))
                link(V.scalar_tensor_tensor(gtmp[:, 1, :], g, -1.0, g, ALU.mult, ALU.max))
                link(V.tensor_scalar(gtmp[:, 1, :], gtmp[:, 1, :], 0.25, None, ALU.max))
                ins = V.scalar_tensor_tensor(g, gtmp[:, 0, :], -1.0, gtmp[:, 1, :], ALU.add, ALU.mult)
                if y == 0:
                    link(ins)
                    dve.wait_ge(s_const, 160)
                    ins = V.tensor_tensor(g[:, D:2 * D], g[:, D:2 * D], down_s[:, :], ALU.mult)
                ins.then_inc(s_mod, 1)

            def stats_of(q, tc):
                if q == 0:
                    dve.wait_ge(s_x, 16 * NCH)
                elif q % 2 == 1:
                    dve.wait_ge(s_xa, 4 * (q + 1))
                else:
                    dve.wait_ge(s_xd, NT)
                j = q * NCH + tc
                for t in range(TPC):
                    ins = V.bn_stats(stats[:, t, :], x_sb[:, tc * TPC + t, :])
                link(ins)
                if j >= 2:
                    dve.wait_ge(s_xh, j - 1)
                    dve.wait_ge(s_rstd, j - 1)
                for t in range(TPC):
                    ins = V.bn_aggr(mv[:, tc % 2, t, :], stats[:, t, :])
                ins.then_inc(s_mv, 1)
                dve.wait_ge(s_mv, j + 1)

            def normed(q, tc):
                j = q * NCH + tc
                dve.wait_ge(s_rstd, j + 1)
                if j >= 2:
                    dve.wait_ge(s_tr, 2 * (j - 1))
                for t in range(TPC):
                    ins = V.tensor_scalar(xh[:, tc % 2, t, :], x_sb[:, tc * TPC + t, :], mv[:, tc % 2, t, 0:1],
                                          rstd[:, tc % 2, t:t + 1], ALU.subtract, ALU.mult)
                ins.then_inc(s_xh, 1)

            def ln(q):
                stats_of(q, 0)
                for tc in range(NCH):
                    if tc + 1 < NCH:
                        stats_of(q, tc + 1)
                    normed(q, tc)

            def qkv(y):
                dve.wait_ge(s_wattn, 128 * (y + 1))
                V.tensor_scalar(b_col[:, :], b_colr[:, :], SCALES[y], None, ALU.mult).then_inc(s_bs, 1)
                if y == 1:
                    dve.wait_ge(s_dn, NT)
                link(V.memset(v_sb[:, :, :, HD], 1.0))
                for k in range(16 * y, 16 * y + 16):
                    b = k % 3
                    dve.wait_ge(s_h, k + 1)
                    link(V.tensor_tensor(st_r[b], st_f[b], st_p[b][:, 0, :], ALU.subtract))
                    link(V.tensor_copy(st_p[b][:, 1, :], st_r[b]))
                    V.tensor_tensor(st_p[b][:, 2, :], st_r[b], st_p[b][:, 1, :], ALU.subtract).then_inc(s_l, 1)
                for t in range(NT):
                    v = y * NT + t
                    dve.wait_ge(s_vp, v + 1)
                    V.tensor_tensor(v_sb[:, t, :, 0:HD], bank(4 + v % 2)[:, 0:D].rearrange("p (h c) -> p h c", h=H),
                                    b_v[:, :].rearrange("p (h c) -> p h c", h=H), ALU.add).then_inc(s_ve, 1)

            def attention(y):
                mb = [M0[y]]

                def reduce_block(n, h, r, q):
                    b = mb[0]
                    mb[0] += 1
                    chunks = n // NG + 1 if CAUSAL[y] else NCH
                    last = CAUSAL[y] and q == n // NG
                    w = (r + 1) * P if last else CH
                    dve.wait_ge(s_mb, b + 1)
                    V.tensor_reduce(mpart[:, h * TPC + r, q:q + 1], bank(4 + b % 2)[:, 0:w], AX.X, ALU.max).then_inc(s_mr, 1)
                    if (h, r, q) == (HG - 1, TPC - 1, chunks - 1):
                        dve.wait_ge(s_mr, b + 1)
                        u = y * NU + n
                        link(V.tensor_reduce(mx[:, :], mpart[:, :, 0:chunks], AX.X, ALU.max))
                        link(V.tensor_scalar(mx[:, :], mx[:, :], ROUND, -ROUND, ALU.add, ALU.add))
                        if u:
                            dve.wait_ge(s_mt, u)
                        link(V.tensor_scalar(mp[:, :, 0], mx[:, :], -1.0, None, ALU.mult))
                        V.scalar_tensor_tensor(mp[:, :, 1], mx[:, :], -1.0, mp[:, :, 0], ALU.mult, ALU.subtract).then_inc(s_mp, 1)

                def normalise(n):
                    u = y * NU + n
                    if n % NG == 0 and n > 0:
                        dve.wait_ge(s_op, 8 * y + 2 * (n // NG))
                    dve.wait_ge(s_oc, u + 1)
                    link(V.stream_shuffle(den[:, :], out_sb[:, :], [HD] * 32))
                    link(V.reciprocal(den[:, :], den[:, :]))
                    V.tensor_tensor(attn_t[:, n % NG, :], out_sb[:, :], den[:, :], ALU.mult).then_inc(s_on, 1)

                def add_output(i, half_):
                    j = 8 * y + 2 * i + half_
                    dve.wait_ge(s_obg, y + 1)
                    dve.wait_ge(s_op, j + 1)
                    t = TPC * i + 2 * half_
                    V.tensor_tensor(x_sb[:, t:t + 2, :], bank(7).rearrange("p (t d) -> p t d", t=2), x_sb[:, t:t + 2, :],
                                    ALU.add).then_inc(s_xa, 1)

                for b in plans[y][0]:
                    reduce_block(*b)
                for s, n, k, blocks in slot_walk(y):
                    if s >= 0 and oproj_slot(n, k):
                        add_output(*oproj_slot(n, k))
                    for b in blocks:
                        reduce_block(*b)
                    if s >= 0 and k == 2 and n > 0:
                        normalise(n - 1)
                normalise(NU - 1)
                add_output(NCH - 1, 0)
                add_output(NCH - 1, 1)

            def router():
                dve.wait_ge(s_le, 1)
                link(V.tensor_scalar(r_s[:, :, :], r_s[:, :, :], 1.0, None, ALU.add))
                link(V.reciprocal(r_s[:, :, :], r_s[:, :, :]))
                mine = r_s[:, :, :].unsqueeze(3).to_broadcast([P, NT, NE, NE])
                other = r_s[:, :, :].unsqueeze(2).to_broadcast([P, NT, NE, NE])
                low = tri[:, :, :].unsqueeze(1).to_broadcast([P, NT, NE, NE])
                link(V.tensor_tensor(r_gt[:, :, :, :], other, mine, ALU.is_gt))
                link(V.tensor_tensor(r_eq[:, :, :, :], other, mine, ALU.is_equal))
                link(V.tensor_tensor(r_eq[:, :, :, :], r_eq[:, :, :, :], low, ALU.mult))
                link(V.tensor_tensor(r_gt[:, :, :, :], r_gt[:, :, :, :], r_eq[:, :, :, :], ALU.add))
                link(V.tensor_reduce(r_rank[:, :, :], r_gt[:, :, :, :], AX.X, ALU.add))
                link(V.tensor_scalar(r_rank[:, :, :], r_rank[:, :, :], 2.0, None, ALU.is_lt))
                link(V.tensor_tensor(r_w[:, :, :], r_rank[:, :, :], r_s[:, :, :], ALU.mult))
                link(V.tensor_reduce(r_sum, r_w[:, :, :], AX.X, ALU.add))
                link(V.tensor_scalar(r_sum, r_sum, 1e-20, None, ALU.add))
                link(V.reciprocal(r_inv, r_sum))
                link(V.tensor_scalar(r_inv, r_inv, 2.5, None, ALU.mult))
                link(V.tensor_tensor(r_w[:, :, :], r_w[:, :, :], r_inv.unsqueeze(2).to_broadcast([P, NT, NE]), ALU.mult))
                link(V.tensor_copy(r_p[:, :, 0, :], r_w[:, :, :]))
                link(V.tensor_tensor(r_lo[:, :, :], r_w[:, :, :], r_p[:, :, 0, :], ALU.subtract))
                link(V.tensor_copy(r_p[:, :, 1, :], r_lo[:, :, :]))
                V.tensor_tensor(r_p[:, :, 2, :], r_lo[:, :, :], r_p[:, :, 1, :], ALU.subtract).then_inc(s_rp, 1)
                for tc in range(NCH):
                    dve.wait_ge(s_rt, tc + 1)
                    V.tensor_copy(wT[0:3 * NE, tc * CH:(tc + 1) * CH], psum[0:3 * NE, 4 + tc % 2, :]).then_inc(s_wt, 1)

            def ffn(y):
                if y == 1:
                    router()
                for what, tc, c in ffn_walk(y):
                    if what == "hid":
                        k = K0[y] + tc * NC[y] + c
                        f = fsize(y, c)
                        dve.wait_ge(s_sil, k + 1)
                        dve.wait_ge(s_u, k + 1)
                        if c == 0 and tc >= 2:
                            dve.wait_ge(s_dn, y * NT + (tc - 1) * TPC)
                        dst, up = hid[tc % 2][0:f, c, :], psum[0:f, 2 + k % 2, :]
                        if y == 0:
                            V.scalar_tensor_tensor(dst, up, up_s[0:f, c:c + 1], sil[k % 2][0:f, :], ALU.mult, ALU.mult).then_inc(s_hid, 1)
                        elif c < RC:
                            link(V.tensor_tensor(utmp[k % 2], up, sil[k % 2], ALU.mult))
                            V.tensor_tensor(dst, bank(4 + k % 2), utmp[k % 2], ALU.mult).then_inc(s_hid, 1)
                        else:
                            V.tensor_tensor(dst, up, sil[k % 2][0:f, :], ALU.mult).then_inc(s_hid, 1)
                    else:
                        for r in range(TPC):
                            j = y * NT + tc * TPC + r
                            dve.wait_ge(s_dn, j + 1)
                            t = tc * TPC + r
                            V.tensor_tensor(x_sb[:, t, :], bank(6 + j % 2)[:, 0:D], x_sb[:, t, :], ALU.add).then_inc(s_xd, 1)

            for y in range(NLAY):
                ln(2 * y)
                qkv(y)
                attention(y)
                ln(2 * y + 1)
                ffn(y)


def constants():
    bf = np.dtype("bfloat16")
    t = np.arange(T)
    i = np.arange(P)
    col = np.ones((CR, HG, T), np.float32)
    col[2], col[4] = t // 256 * 256, t % 256
    row0 = np.zeros((CR, HG, T), np.float32)
    row0[2], row0[3], row0[4], row0[5] = 1, -(t // 256 * 256), 1, -(t % 256)
    e = np.arange(NE)
    esel = np.zeros((3 * NE, RC, P), np.float32)
    for f in range(NE * FE):
        esel[f // FE::NE, f // P, f % P] = 1
    return {
        "ident": np.eye(P, dtype=np.float32), "identb": np.eye(P).astype(bf),
        "neg_m": np.where(i[None, :] > i[:, None], -1e30, 0).astype(bf),
        "neg_e": np.where(i[:, None] > i[None, :], -1e30, 0).astype(bf),
        "col_const": col.astype(bf), "row_const0": row0.astype(bf), "row_const1": np.zeros((CR, HG, T), bf),
        "tri": (e[None, :] < e[:, None]).astype(np.float32), "esel": esel.astype(bf),
    }


def laid_out(v):
    v = {k: np.asarray(x) for k, x in v.items()}

    def columns(b):
        n = -(-b.shape[0] // P)
        out = np.zeros((n * P,), b.dtype)
        out[:b.shape[0]] = b
        return np.ascontiguousarray(out.reshape(n, P).T)

    def padded(w):
        out = np.zeros((NG, HG, 32, D), w.dtype)
        out[:, :, 0:HD] = w.reshape(NG, HG, HD, D)
        return out.reshape(NG * P, D)

    c = np.concatenate([v["L0_c"].reshape(KD, P), v["L1_c"].reshape(KD, P)]).T
    a = {
        "x": v["L0_attn_x"].reshape(T, D), "c": c, "wmod0": v["L0_wmod"], "wmod1": v["L1_wmod"],
        "w_row0": v["L0_attn_k_w"].T, "w_col0": v["L0_attn_q_w"].T, "w_v0": v["L0_attn_v_w"].T,
        "b_row0": columns(v["L0_attn_k_b"]), "b_col0": columns(v["L0_attn_q_b"]),
        "b_v0": v["L0_attn_v_b"], "b_o0": v["L0_attn_o_b"], "w_o0": padded(v["L0_attn_o_w"].T),
        "w_row1": v["L1_attn_wq"], "w_col1": v["L1_attn_wk"], "w_v1": v["L1_attn_wv"],
        "b_row1": columns(v["L1_attn_bq"]), "b_col1": columns(v["L1_attn_bk"]),
        "b_v1": v["L1_attn_bv"], "b_o1": v["L1_attn_bo"], "w_o1": padded(v["L1_attn_wo"]),
        "w_gate0": v["L0_ffn_gate_w"].T, "w_up0": v["L0_ffn_up_w"].T, "w_down0": v["L0_ffn_down_w"].T,
        "gate_s": columns(v["L0_ffn_gate_s"]), "up_s": columns(v["L0_ffn_up_s"]), "down_s": v["L0_ffn_down_s"],
        "w_gate1": np.concatenate([v["L1_ffn_exp_wg"].reshape(NE * FE, D), v["L1_ffn_shared_wg"]]).T,
        "w_up1": np.concatenate([v["L1_ffn_exp_wu"].reshape(NE * FE, D), v["L1_ffn_shared_wu"]]).T,
        "w_down1": np.concatenate([v["L1_ffn_exp_wd"].transpose(0, 2, 1).reshape(NE * FE, D), v["L1_ffn_shared_wd"].T]),
        "gate_w": v["L1_ffn_gate_w"].T,
    }
    return {k: np.ascontiguousarray(x) for k, x in {**a, **constants()}.items()}


def kernel(**inputs):
    import concourse.bacc as bacc
    from concourse.bass_utils import run_bass_kernel_spmd

    arrays = laid_out(inputs)
    nc = bacc.Bacc("TRN2", target_bir_lowering=False, num_devices=1)
    aps = {k: nc.dram_tensor(f"in_{k}", x.shape, mybir.dt.from_np(x.dtype), kind="ExternalInput").ap()
           for k, x in arrays.items()}
    aps["out"] = nc.dram_tensor("out", (T, D), F32, kind="ExternalOutput").ap()
    adaln_two_layers(nc, aps)
    got = run_bass_kernel_spmd(nc, [{f"in_{k}": x for k, x in arrays.items()}], core_ids=[0])
    return got.results[0]["out"].reshape(1, T, D)
```

```python
from contextlib import ExitStack

import numpy as np
import concourse.bass as bass
from concourse import mybir

F32 = mybir.dt.float32
BF16 = mybir.dt.bfloat16
ALU = mybir.AluOpType
ACT = mybir.ActivationFunctionType
AX = mybir.AxisListType

P = 128
T = 2048
D = 256
KD = D // P
NT = T // P
CH = 512
NCH = T // CH
TPC = CH // P
H = 16
HD = D // H
HG = 4
NG = H // HG
GF = HG * HD
VW = HD + 1
SLOTS_ROW = (0, 0, 1, 1, 0, 2)
SLOTS_COL = (0, 1, 0, 1, 2, 0)
CR = 6
KS = CR + HD * len(SLOTS_ROW)
SCALES = (HD ** -0.5, D ** -0.5)
ROUND = 12582912.0
EPS = 1e-5
NE = 8
FE = 176
F0 = 704
F1 = NE * FE + 2 * FE
FS = (F0, F1)
NC = tuple(-(-f // P) for f in FS)
RC = NE * FE // P
ROUTE = ((0, 3 * NT // 4), (3 * NT // 4, NT))
LB, WB = (4, 6), (5, 7)
CAUSAL = (True, False)
NLAY = 2


def fsize(layer, c):
    return min(P, FS[layer] - P * c)


def steps_of(layer, n):
    return TPC * (n // NG + 1) if CAUSAL[layer] else NT


def plan(layer):
    units = NCH * NG
    blocks, ends = [], []
    for n in range(units):
        chunks = n // NG + 1 if CAUSAL[layer] else NCH
        blocks += [(n, h, r, q) for h in range(HG) for r in range(TPC) for q in range(chunks)]
        ends.append(len(blocks))
    start = [sum(steps_of(layer, m) for m in range(n)) for n in range(units)]
    total = start[-1] + steps_of(layer, units - 1)
    slots, done = [], ends[0]
    first = blocks[:done]
    for s in range(-1, total):
        want = len(blocks)
        for n in range(1, units):
            a, b = start[n - 1] - 4, start[n] - 4
            if a <= s < b:
                want = ends[n - 1] + (ends[n] - ends[n - 1]) * (s - a) // (b - a)
        want = max(want, done)
        slots.append(blocks[done:want])
        done = want
    return first, slots, start, total


def adaln_two_layers(nc, a):
    ctx = ExitStack()
    with ctx:
        def sb(name, shape, dt=F32):
            return ctx.enter_context(nc.sbuf_tensor(name, shape, dt))

        def sem(name):
            return ctx.enter_context(nc.semaphore(name))

        x_sb = sb("x_sb", [P, NT, D])
        key_region = sb("key_region", [P, H * T // 2])
        v_region = sb("v_region", [P, NT * H * VW])
        row_region = sb("row_region", [P, NG * HG * CH // 2])
        probs = sb("probs", [P, 2, HG, CH])
        hT = sb("hT", [P, KD, T])
        attn_region = sb("attn_region", [P, 2 * KD * CH])
        ffn_w = sb("ffn_w", [P, 2, KD * F1])
        w_row = sb("w_row", [P, KD, D])
        w_col = sb("w_col", [P, KD, D])
        w_v = sb("w_v", [P, KD, D])
        w_o = sb("w_o", [P, KD, D])
        b_row = sb("b_row", [P, KD])
        b_col = sb("b_col", [P, KD])
        b_colr = sb("b_colr", [P, KD])
        b_v = sb("b_v", [P, D])
        b_o = sb("b_o", [P, D])
        out_sb = sb("out_sb", [P, CH])
        rden = sb("rden", [P, TPC, HG])
        mrow_t = sb("mrow_t", [P, CH], BF16)
        mpart = sb("mpart", [P, HG * TPC, NCH])
        mx = sb("mx", [P, HG * TPC])
        mp = sb("mp", [P, HG * TPC, 32], BF16)
        ident = sb("ident", [P, P])
        identb = sb("identb", [P, P], BF16)
        neg_m = sb("neg_m", [P, P], BF16)
        neg_e = sb("neg_e", [P, P], BF16)
        gab = sb("gab", [P, NLAY, 2 * D])
        modc = sb("modc", [P, NLAY, 8])
        stats = sb("stats", [P, TPC, 6])
        mv = sb("mv", [P, 2, TPC, 2])
        rstd = sb("rstd", [P, 2, TPC])
        vare = sb("vare", [P, TPC])
        half = sb("half", [P, TPC])
        c_sb = sb("c_sb", [P, 2 * KD])
        ce = sb("ce", [P, 2 * KD])
        cs = sb("cs", [P, 2 * KD])
        gate_s = sb("gate_s", [P, NC[0]])
        up_s = sb("up_s", [P, NC[0]])
        down_s = sb("down_s", [P, D])
        gate_w = sb("gate_w", [P, KD, NE])
        tri = sb("tri", [P, NE, NE])
        esel = sb("esel", [3 * NE, RC, P], BF16)

        keys = key_region[:, :].bitcast(BF16).rearrange("p (h t) -> p h t", h=H)
        v_sb = v_region[:, :].rearrange("p (t h c) -> p t h c", t=NT, h=H)
        rows = row_region[:, :].bitcast(BF16).rearrange("p (g h t) -> p g h t", g=NG, h=HG)
        attn_n = attn_region[:, 0:TPC * D].rearrange("p (t d) -> p t d", t=TPC)
        attn_t = attn_region[:, TPC * D:].rearrange("p (k t) -> p k t", k=KD)
        wmod = key_region[:, 0:KD * 6 * D * NLAY].rearrange("p (l k n) -> p l k n", l=NLAY, k=KD)
        o1 = KD * 6 * D * NLAY
        csb = key_region[:, o1:o1 + 2 * KD * P].rearrange("p (k n) -> p k n", k=2 * KD)
        o1 += 2 * KD * P
        gtmp = key_region[:, o1:o1 + 3 * 2 * D].rearrange("p (k n) -> p k n", k=3)
        SW = CH * 2 + 3 * CH // 2
        stage = [key_region[:, o:o + SW] for o in (NC[0] * CH, NC[0] * CH + SW, (NC[1] + NC[0]) * CH)]
        st_f = [s[:, 0:CH] for s in stage]
        st_r = [s[:, CH:2 * CH] for s in stage]
        st_p = [s[:, 2 * CH:SW].bitcast(BF16).rearrange("p (k t) -> p k t", k=3) for s in stage]
        xh = attn_region[:, :].rearrange("p (b t d) -> p b t d", b=2, t=TPC)
        HW = NC[1] * CH
        hid = [key_region[:, b * HW:(b + 1) * HW].rearrange("p (c t) -> p c t", c=NC[1]) for b in range(2)]
        sil = [key_region[:, 2 * HW + b * CH:2 * HW + (b + 1) * CH] for b in range(2)]
        utmp = [key_region[:, 2 * HW + (2 + b) * CH:2 * HW + (3 + b) * CH] for b in range(2)]
        down = v_region[:, 0:NC[1] * D].rearrange("p (c d) -> p c d", c=NC[1])
        up_gate = [[ffn_w[:, i, 0:KD * FS[y]].rearrange("p (k f) -> p k f", k=KD) for i in range(2)]
                   for y in range(NLAY)]
        ro = [0]

        def take(n):
            ro[0] += n
            return row_region[:, ro[0] - n:ro[0]]

        r_s = take(NT * NE).rearrange("p (t e) -> p t e", t=NT)
        r_gt = take(NT * NE * NE).rearrange("p (t e f) -> p t e f", t=NT, e=NE)
        r_eq = take(NT * NE * NE).rearrange("p (t e f) -> p t e f", t=NT, e=NE)
        r_rank = take(NT * NE).rearrange("p (t e) -> p t e", t=NT)
        r_w = take(NT * NE).rearrange("p (t e) -> p t e", t=NT)
        r_sum = take(NT)
        r_inv = take(NT)
        r_lo = take(NT * NE).rearrange("p (t e) -> p t e", t=NT)
        r_p = take(NT * 3 * NE // 2).bitcast(BF16).rearrange("p (t k e) -> p t k e", t=NT, k=3)
        wT = take(T // 2).bitcast(BF16)

        psum = ctx.enter_context(nc.psum_tensor("psum", [P, 8, CH], F32))

        def bank(b):
            return psum[:, b, :]

        parts = nc.dram_tensor("parts", (2, 3, D, T), BF16, kind="Internal").ap()

        s_x = sem("x_loaded")
        s_const = sem("constants_loaded")
        s_wmod = sem("modulation_inputs_loaded")
        s_wattn = sem("attention_weights_loaded")
        s_wffn = sem("ffn_weights_loaded")
        s_wdown = sem("down_weights_loaded")
        s_dve = sem("vector_chain")
        s_act = sem("scalar_chain")
        s_pool = sem("gpsimd_chain")
        s_ce = sem("exp_c_done")
        s_cs = sem("silu_c_spread")
        s_modp = sem("modulation_product")
        s_mod = sem("modulation_ready")
        s_wo = sem("output_weights_scaled")
        s_wd = sem("down_weights_scaled")
        s_obg = sem("output_bias_added")
        s_mv = sem("ln_stats_ready")
        s_rstd = sem("ln_rstd_ready")
        s_xh = sem("normed_ready")
        s_tr = sem("normed_transposed")
        s_hte = sem("h_ready")
        s_pj = sem("projection_product")
        s_qf = sem("projection_evacuated")
        s_bs = sem("column_bias_scaled")
        s_h = sem("high_part_ready")
        s_l = sem("low_part_ready")
        s_split = [sem(f"parts_stored{b}") for b in range(3)]
        s_vp = sem("value_product")
        s_ve = sem("values_ready")
        s_key = [sem(f"keys_loaded{g}") for g in range(NG)]
        s_row = [sem(f"rows_loaded{g}") for g in range(NG)]
        s_mb = sem("max_block_product")
        s_mr = sem("max_block_reduced")
        s_mp = sem("max_parts_ready")
        s_mt = sem("max_transposed")
        s_mtc = sem("max_rows_copied")
        s_mrow = sem("max_rows_placed")
        s_e = sem("scores_ready")
        s_p = sem("probs_ready")
        s_pv = sem("probs_used")
        s_oc = sem("attn_copied")
        s_ft = sem("sums_transposed")
        s_on = sem("attn_normalised")
        s_bt = sem("attn_transposed")
        s_ac = sem("attn_features_copied")
        s_op = sem("output_product")
        s_xa = sem("attn_added")
        s_g = sem("gate_product")
        s_u = sem("up_product")
        s_sil = sem("silu_ready")
        s_hid = sem("hidden_ready")
        s_dn = sem("down_product")
        s_xd = sem("ffn_added")
        s_lg = sem("router_product")
        s_le = sem("router_exp")
        s_rp = sem("router_parts_ready")
        s_rt = sem("router_transposed")
        s_wt = sem("router_rows_ready")
        s_out = sem("output_stored")

        plans = [plan(y) for y in range(NLAY)]
        STEPS = [p[3] for p in plans]
        S0 = [0, STEPS[0], STEPS[0] + STEPS[1]]
        MB = [sum(len(s) for s in p[1]) + len(p[0]) for p in plans]
        M0 = [0, MB[0], MB[0] + MB[1]]
        NU = NCH * NG
        K0 = [0, NC[0] * NCH, (NC[0] + NC[1]) * NCH]

        def slot_walk(y):
            first, slots, start, total = plans[y]
            for s in range(-1, total):
                n = max(m for m in range(NU) if start[m] <= max(s, 0))
                yield s, n, s - start[n], slots[s + 1]

        def unit_steps(y, n):
            return S0[y] + plans[y][2][n] + steps_of(y, n)

        def mt_slot(y, n, k):
            return n + 1 if n + 1 < NU and k == steps_of(y, n) - 3 else None

        def oproj_slot(n, k):
            return (n // NG - 1, k - 4) if n % NG == 0 and n > 0 and k in (4, 5) else None

        def back_slot(n, k):
            return (n // NG - 1, k - 2) if n % NG == 0 and n > 0 and k in (2, 3) else None

        def ln_slot(n, k):
            return (n // NG - 1, k - 2) if n % NG == 1 and n > 1 and k in (2, 3) else None

        def ln_bank(q, tc, c):
            if q == 0:
                return c
            if q == 2:
                return 4 + c
            return 6 if tc < NCH - 1 else 6 + c

        def ffn_walk(y):
            seq = []
            if y == 0:
                for tc in range(NCH):
                    for c in range(NC[0]):
                        seq.append(("hid", tc, c))
                        if tc == 0 and c < 5:
                            seq.append(("tail", 0, c))
                        if (tc, c) == (1, 0):
                            seq.append(("ln", NCH - 1, 0))
                        if tc > 0 and c in (1, 3, 4):
                            seq.append(({1: "down", 3: "ln", 4: "proj"}[c], tc - 1, 0))
                seq += [(w, NCH - 1, 0) for w in ("down", "ln", "proj")]
            else:
                shared, routed = list(range(RC, NC[1])), list(range(RC))
                seq.append(("logits", 0, 0))
                for m, (tc, c) in enumerate([(tc, c) for tc in range(2) for c in shared]):
                    seq.append(("hid", tc, c))
                    if m < 5:
                        seq.append(("tail", 0, m))
                    if m == 4:
                        seq.append(("weights", 0, 0))
                seq += [("hid", 0, c) for c in routed[:1]] + [("ln", NCH - 1, 0)]
                seq += [("hid", 0, c) for c in routed[1:3]] + [("logits", 1, 0)]
                seq += [("hid", 0, c) for c in routed[3:7]] + [("weights", 1, 0)]
                seq += [("hid", 0, c) for c in routed[7:]]
                seq += [("hid", 1, c) for c in routed[:2]] + [("down", 0, 0)] + [("hid", 1, c) for c in routed[2:]]
                for tc in range(2, NCH):
                    order = shared + routed
                    seq += [("hid", tc, c) for c in order[:2]] + [("down", tc - 1, 0)] + [("hid", tc, c) for c in order[2:]]
                seq.append(("down", NCH - 1, 0))
            done = K0[y]
            last = {}
            for what, tc, c in seq:
                if what == "hid":
                    last[tc] = done + 1
                    yield what, tc, c, done
                    done += 1
                else:
                    yield what, tc, c, last.get(tc, done) if what == "down" else done

        def ln_of(y, tc, k):
            return 2 * y + 1 if y or tc == NCH - 1 and k <= K0[y] + NC[0] + 1 else 2

        def xh_buf(q, tc):
            return 1 if q % 2 else tc % 2

        def hid_end(y, tc):
            return max(k + 1 for what, t, _c, k in ffn_walk(y) if what == "hid" and t == tc)

        block = ctx.enter_context(nc.Block())

        @block.sync
        def _(sp):
            def load_attn(y):
                for dst, name in ((w_row, "w_row"), (w_col, "w_col"), (w_v, "w_v")):
                    sp.dma_start(dst[:, :, :], a[f"{name}{y}"].rearrange("(k p) n -> p k n", p=P)).then_inc(s_wattn, 16)
                sp.dma_start(w_o[:, :, :], a[f"w_o{y}"].rearrange("(k p) n -> p k n", p=P)).then_inc(s_wattn, 16)
                sp.dma_start(b_row[:, :], a[f"b_row{y}"]).then_inc(s_wattn, 16)
                sp.dma_start(b_colr[:, :], a[f"b_col{y}"]).then_inc(s_wattn, 16)
                sp.dma_start(b_v[:, :], a[f"b_v{y}"].partition_broadcast(P)).then_inc(s_wattn, 16)
                sp.dma_start(b_o[:, :], a[f"b_o{y}"].partition_broadcast(P)).then_inc(s_wattn, 16)

            def load_ffn(y):
                for i, name in enumerate(("w_gate", "w_up")):
                    sp.dma_start(up_gate[y][i], a[f"{name}{y}"].rearrange("(k p) n -> p k n", p=P)).then_inc(s_wffn, 16)

            def load_down(y):
                full = FS[y] // P
                sp.dma_start(down[:, 0:full, :], a[f"w_down{y}"][0:full * P, :].rearrange("(c p) d -> p c d", p=P)).then_inc(s_wdown, 16)
                sp.dma_start(down[0:FS[y] - full * P, full, :], a[f"w_down{y}"][full * P:FS[y], :]).then_inc(s_wdown, 16)

            def load_rows(y, n):
                i, g = n // NG, n % NG
                if n >= NG:
                    sp.wait_ge(s_e, HG * unit_steps(y, n - NG))
                sp.dma_start(rows[0:CR, g, :, :], a[f"row_const{y}"][:, :, i * CH:(i + 1) * CH]).then_inc(s_row[g], 16)
                for k, part in enumerate(SLOTS_ROW):
                    src = parts[0, part, g * GF:(g + 1) * GF, i * CH:(i + 1) * CH].rearrange("(h c) t -> c h t", c=HD)
                    sp.dma_start(rows[CR + HD * k:CR + HD * (k + 1), g, :, :], src).then_inc(s_row[g], 16)

            def load_keys(g):
                sp.dma_start(keys[0:CR, g * HG:(g + 1) * HG, :], a["col_const"]).then_inc(s_key[g], 16)
                for k, part in enumerate(SLOTS_COL):
                    src = parts[1, part, g * GF:(g + 1) * GF, :].rearrange("(h c) t -> c h t", c=HD)
                    sp.dma_start(keys[CR + HD * k:CR + HD * (k + 1), g * HG:(g + 1) * HG, :], src).then_inc(s_key[g], 16)

            sp.dma_start(c_sb[:, :], a["c"]).then_inc(s_wmod, 16)
            for tc in range(NCH):
                sp.dma_start(x_sb[:, tc * TPC:(tc + 1) * TPC, :],
                             a["x"][tc * CH:(tc + 1) * CH, :].rearrange("(t p) d -> p t d", p=P)).then_inc(s_x, 16)
            for y in range(NLAY):
                sp.dma_start(wmod[:, y, :, :], a[f"wmod{y}"].rearrange("(k p) n -> p k n", p=P)).then_inc(s_wmod, 16)
            load_attn(0)
            for dst, name in ((ident, "ident"), (identb, "identb"), (neg_m, "neg_m"), (neg_e, "neg_e"),
                              (gate_s, "gate_s"), (up_s, "up_s")):
                sp.dma_start(dst[:, :], a[name]).then_inc(s_const, 16)
            sp.dma_start(down_s[:, :], a["down_s"].partition_broadcast(P)).then_inc(s_const, 16)
            sp.dma_start(gate_w[:, :, :], a["gate_w"].rearrange("(k p) n -> p k n", p=P)).then_inc(s_const, 16)
            sp.dma_start(tri[:, :, :], a["tri"].partition_broadcast(P)).then_inc(s_const, 16)
            sp.dma_start(esel[:, :, :], a["esel"]).then_inc(s_const, 16)
            load_ffn(0)
            for y in range(NLAY):
                for tc in range(NCH):
                    for side in range(2):
                        for f in range(KD):
                            k = (y * NCH + tc) * 4 + side * KD + f
                            sp.wait_ge(s_l, k + 1)
                            sp.dma_start(parts[side, :, f * P:(f + 1) * P, tc * CH:(tc + 1) * CH].rearrange("k f t -> f k t"),
                                         st_p[k % 3]).then_inc(s_split[k % 3], 16)
                for b in range(3):
                    jobs = len([k for k in range(16 * (y + 1)) if k % 3 == b])
                    sp.wait_ge(s_split[b], 16 * jobs)
                for g in range(NG):
                    load_rows(y, g)
                    load_keys(g)
                if y == 1:
                    sp.wait_ge(s_u, K0[1])
                    load_ffn(1)
                for s, n, k, _blocks in slot_walk(y):
                    if k == 0 and n > 0:
                        if n + 3 < NU:
                            load_rows(y, n + 3)
                    m = 0 if s == -1 else mt_slot(y, n, k)
                    if m is not None:
                        sp.wait_ge(s_mtc, y * NU + m + 1)
                        for h in range(HG):
                            sp.dma_start(rows[0:2, m % NG, h, :], mrow_t[32 * h:32 * h + 2, :]).then_inc(s_mrow, 16)
                sp.wait_ge(s_pv, S0[y + 1])
                load_down(y)
                if y == 0:
                    sp.wait_ge(s_op, 8)
                    load_attn(1)
            for t in range(NT):
                sp.wait_ge(s_xd, NT + t + 1)
                sp.dma_start(a["out"][t * P:(t + 1) * P, :], x_sb[:, t, :]).then_inc(s_out, 16)
            sp.wait_ge(s_out, 16 * NT)

        @block.gpsimd
        def _(pool):
            chain = [0]

            def link(ins):
                chain[0] += 1
                ins.then_inc(s_pool, 1)
                pool.wait_ge(s_pool, chain[0])

            def ln(q):
                for tc in range(NCH):
                    j = q * NCH + tc
                    pool.wait_ge(s_mv, j + 1)
                    if j:
                        pool.wait_ge(s_rstd, j)
                    link(nc.gpsimd.tensor_scalar(vare[:, :], mv[:, tc % 2, :, 1], EPS, None, ALU.add))
                    if j >= 2:
                        pool.wait_ge(s_xh, j - 1)
                    nc.gpsimd.tensor_tensor(rstd[:, tc % 2, :], vare[:, :], half[:, :], ALU.pow).then_inc(s_rstd, 1)

            def scale_wo(y):
                pool.wait_ge(s_mod, y + 1)
                pool.wait_ge(s_wattn, 128 * (y + 1))
                for g in range(KD):
                    link(nc.gpsimd.tensor_tensor(w_o[:, g, :], w_o[:, g, :], gab[:, y, 0:D], ALU.mult))
                nc.gpsimd.tensor_tensor(b_o[:, :], b_o[:, :], gab[:, y, 0:D], ALU.mult).then_inc(s_wo, 1)
                pool.wait_ge(s_wo, y + 1)

            def add_bias(y):
                pool.wait_ge(s_xh, (2 * y + 1) * NCH)
                for t in range(NT):
                    ins = nc.gpsimd.tensor_tensor(x_sb[:, t, :], x_sb[:, t, :], b_o[:, :], ALU.add)
                ins.then_inc(s_obg, 1)

            def scale_down(y):
                pool.wait_ge(s_wdown, 32 * (y + 1))
                for c in range(NC[y]):
                    f = fsize(y, c)
                    ins = nc.gpsimd.tensor_tensor(down[0:f, c, :], down[0:f, c, :], gab[0:f, y, D:2 * D], ALU.mult)
                ins.then_inc(s_wd, 1)

            link(nc.gpsimd.memset(half[:, :], -0.5))
            for y in range(NLAY):
                ln(2 * y)
                scale_wo(y)
                add_bias(y)
                ln(2 * y + 1)
                scale_down(y)

        @block.tensor
        def _(pe):
            pe.wait_ge(s_cs, 1)
            pe.wait_ge(s_wmod, 48)
            for y in range(NLAY):
                for i, col in enumerate((2, 5)):
                    for k in range(KD):
                        mm = pe.matmul(bank(2 * y)[:, i * D:(i + 1) * D], csb[:, y * KD + k, :],
                                       wmod[:, y, k, col * D:(col + 1) * D], start=(k == 0), stop=(k == KD - 1))
                for i in range(8):
                    col = (0, 1, 3, 4)[i // 2] * D + (i % 2) * P
                    for k in range(KD):
                        mm = pe.matmul(bank(2 * y + 1)[:, i:i + 1], wmod[:, y, k, col:col + P],
                                       cs[:, y * KD + k:y * KD + k + 1], start=(k == 0), stop=(k == KD - 1))
                mm.then_inc(s_modp, 1)
            pe.wait_ge(s_const, 160)

            def ln(q, tc, c):
                j = q * NCH + tc
                y = q // 2
                pe.wait_ge(s_xh, j + 1)
                if j == 0:
                    pe.wait_ge(s_mod, 1)
                elif q == 0:
                    pe.wait_ge(s_hte, 2 * (j - 1) + c + 1)
                elif q == 2:
                    if tc == 0:
                        pe.wait_ge(s_mr, M0[1])
                    else:
                        pe.wait_ge(s_qf, 4 * (NCH + tc))
                elif tc < NCH - 1:
                    if c == 0:
                        pe.wait_ge(s_on, y * NU + NG * (tc + 1) + 1)
                    else:
                        pe.wait_ge(s_hte, 2 * j + 1)
                else:
                    pe.wait_ge(s_on, (y + 1) * NU)
                    pe.wait_ge(s_xa, 8 * (y + 1))
                for t in range(TPC):
                    mm = pe.transpose(bank(ln_bank(q, tc, c))[:, t * P:(t + 1) * P],
                                      xh[:, xh_buf(q, tc), t, c * P:(c + 1) * P], ident[:, :])
                mm.then_inc(s_tr, 1)

            def proj(y, tc):
                if tc == 0:
                    pe.wait_ge(s_wattn, 128 * (y + 1))
                    pe.wait_ge(s_mod, NLAY)
                pe.wait_ge(s_hte, 16 * y + 2 * (tc + 1))
                tok = slice(tc * CH, (tc + 1) * CH)
                for side, w in enumerate((w_row, w_col)):
                    for f in range(KD):
                        j = (y * NCH + tc) * 4 + side * KD + f
                        if j >= 2:
                            pe.wait_ge(s_qf, j - 1)
                        for k in range(KD):
                            mm = pe.matmul(bank(2 + 2 * y + j % 2), w[:, k, f * P:(f + 1) * P], hT[:, k, tok],
                                           start=(k == 0), stop=(k == KD - 1))
                        mm.then_inc(s_pj, 1)

            def value(y, t):
                v = y * NT + t
                if t == 0:
                    pe.wait_ge(s_qf, 16 * (y + 1))
                if v >= 2:
                    pe.wait_ge(s_ve, v - 1)
                for k in range(KD):
                    mm = pe.matmul(bank(6 + v % 2)[:, 0:D], hT[:, k, t * P:(t + 1) * P], w_v[:, k, :],
                                   start=(k == 0), stop=(k == KD - 1))
                mm.then_inc(s_vp, 1)

            def sums_transpose(y, n):
                pe.wait_ge(s_oc, y * NU + n + 1)
                for t in range(TPC):
                    mm = pe.transpose(bank(6 + n % 2)[:, t * P:(t + 1) * P], out_sb[:, t * P:(t + 1) * P], ident[:, :])
                mm.then_inc(s_ft, 1)

            def back_transpose(y, i, half_):
                pe.wait_ge(s_on, y * NU + NG * (i + 1))
                if half_:
                    pe.wait_ge(s_ac, 2 * (y * NCH + i) + 1)
                for f in range(KD):
                    for r in range(2):
                        mm = pe.transpose(bank(7)[:, (2 * f + r) * P:(2 * f + r + 1) * P],
                                          attn_n[:, 2 * half_ + r, f * P:(f + 1) * P], ident[:, :])
                mm.then_inc(s_bt, 1)

            def output(y, i, half_):
                if half_ == 0:
                    pe.wait_ge(s_ac, 2 * (y * NCH + i) + 2)
                    pe.wait_ge(s_wo, y + 1)
                else:
                    pe.wait_ge(s_xa, 8 * y + 2 * i + 1)
                for r in range(2):
                    t = 2 * half_ + r
                    for f in range(KD):
                        mm = pe.matmul(bank(7)[:, r * D:(r + 1) * D], attn_t[:, f, t * P:(t + 1) * P], w_o[:, f, :],
                                       start=(f == 0), stop=(f == KD - 1))
                mm.then_inc(s_op, 1)

            def attention(y):
                pe.wait_ge(s_qf, 16 * (y + 1))
                mb = [M0[y]]

                def max_block(n, h, r, q):
                    i, g = n // NG, n % NG
                    b = mb[0]
                    mb[0] += 1
                    if (h, r, q) == (0, 0, 0):
                        pe.wait_ge(s_row[g], 112 * (y * NCH + i + 1))
                        pe.wait_ge(s_key[g], 112 * (y + 1))
                    if b >= 3:
                        pe.wait_ge(s_mr, b - 2)
                    last = CAUSAL[y] and q == i
                    w = (r + 1) * P if last else CH
                    out = bank(3 + b % 3)
                    mm = pe.matmul(out[:, 0:w], rows[0:KS, g, h, r * P:(r + 1) * P],
                                   keys[0:KS, g * HG + h, q * CH:q * CH + w], start=True, stop=not last)
                    if last:
                        mm = pe.matmul(out[:, w - P:w], identb[:, :], neg_m[:, :], start=False, stop=True)
                    mm.then_inc(s_mb, 1)

                def max_transpose(n):
                    u = y * NU + n
                    pe.wait_ge(s_mp, u + 1)
                    if n < 2:
                        pe.wait_ge(s_ve, NT * (y + 1))
                    elif n % NG == 1:
                        pe.wait_ge(s_xa, 8 * y + 2 * (n // NG))
                    elif n % NG == 2 and n > 2:
                        pe.wait_ge(s_hte, 16 * y + 8 + 2 * (n // NG))
                    elif n >= 2:
                        pe.wait_ge(s_on, u - 1)
                    for h in range(HG):
                        for r in range(TPC):
                            mm = pe.matmul(psum[32 * h:32 * h + 32, 6 + n % 2, r * P:(r + 1) * P],
                                           mp[:, h * TPC + r, :], identb[:, :], start=True, stop=True)
                    mm.then_inc(s_mt, 1)

                def scores(s, n, jt, h):
                    i, g = n // NG, n % NG
                    e = HG * (S0[y] + s) + h
                    if jt == 0 and h == 0:
                        pe.wait_ge(s_mrow, 64 * (y * NU + n + 1))
                    if e >= 3:
                        pe.wait_ge(s_p, e - 2)
                    off = max(0, jt - TPC * i) * P if CAUSAL[y] else 0
                    diag = CAUSAL[y] and jt >= TPC * i
                    out = bank(e % 3)
                    mm = pe.matmul(out[:, off:CH], keys[0:KS, g * HG + h, jt * P:(jt + 1) * P],
                                   rows[0:KS, g, h, off:CH], start=True, stop=not diag)
                    if diag:
                        mm = pe.matmul(out[:, off:off + P], identb[:, :], neg_e[:, :], start=False, stop=True)
                    mm.then_inc(s_e, 1)

                def values(s, n, jt):
                    i, g = n // NG, n % NG
                    pe.wait_ge(s_p, HG * (S0[y] + s + 1))
                    if jt == 0:
                        pe.wait_ge(s_mtc, y * NU + n + 1)
                    off = max(0, jt - TPC * i) * P if CAUSAL[y] else 0
                    for h in range(HG):
                        mm = pe.matmul(psum[32 * h:32 * h + VW, 6 + n % 2, off:CH], v_sb[:, jt, g * HG + h, :],
                                       probs[:, (S0[y] + s) % 2, h, off:CH], start=(jt == 0), stop=(jt == steps_of(y, n) - 1))
                    mm.then_inc(s_pv, 1)

                first = plans[y][0]
                if y == 0:
                    pe.wait_ge(s_hte, 2 * NCH)
                for t in range(NT // 2):
                    value(y, t)
                for m, b in enumerate(first):
                    max_block(*b)
                    if (m + 1) % (len(first) // (NT // 2)) == 0:
                        value(y, NT // 2 + (m + 1) // (len(first) // (NT // 2)) - 1)
                before = None
                for s, n, k, blocks in slot_walk(y):
                    if s == -1:
                        max_transpose(0)
                    quarter = [len(blocks) * m // 4 for m in range(5)]
                    for m in range(4):
                        for b in blocks[quarter[m]:quarter[m + 1]]:
                            max_block(*b)
                        if m % 2 == 0 and s >= 0:
                            scores(s, n, k, m)
                            scores(s, n, k, m + 1)
                        if m == 1 and before:
                            values(*before)
                    before = (s, n, k) if s >= 0 else None
                    if s >= 0:
                        if k == 1 and n > 0:
                            sums_transpose(y, n - 1)
                        if back_slot(n, k):
                            back_transpose(y, *back_slot(n, k))
                        if oproj_slot(n, k):
                            output(y, *oproj_slot(n, k))
                        if ln_slot(n, k):
                            ln(2 * y + 1, *ln_slot(n, k))
                        if mt_slot(y, n, k) is not None:
                            max_transpose(mt_slot(y, n, k))
                values(*before)

            def logits(part):
                lo, hi = ROUTE[part]
                pe.wait_ge(s_hte, 24 + 2 * (hi // TPC))
                for t in range(lo, hi):
                    for k in range(KD):
                        mm = pe.matmul(bank(LB[part])[:, t * NE:(t + 1) * NE], hT[:, k, t * P:(t + 1) * P], gate_w[:, k, :],
                                       start=(k == 0), stop=(k == KD - 1))
                mm.then_inc(s_lg, 1)

            def weights(part):
                pe.wait_ge(s_rp, part + 1)
                for tc in range(ROUTE[part][0] // TPC, ROUTE[part][1] // TPC):
                    if tc:
                        pe.wait_ge(s_wt, tc)
                    for r in range(TPC):
                        t = tc * TPC + r
                        mm = pe.matmul(psum[0:3 * NE, WB[part], r * P:(r + 1) * P],
                                       r_p[:, t, :, :].rearrange("p k e -> p (k e)"), identb[:, :], start=True, stop=True)
                    mm.then_inc(s_rt, 1)

            def ffn(y):
                pe.wait_ge(s_wffn, 32 * (y + 1))
                pe.wait_ge(s_mr, M0[y + 1])
                for what, tc, c, k in ffn_walk(y):
                    tok = slice(tc * CH, (tc + 1) * CH)
                    if what == "hid":
                        f = fsize(y, c)
                        pe.wait_ge(s_hte, 16 * y + 8 + 2 * (tc + 1))
                        if k - K0[y] >= 2:
                            pe.wait_ge(s_sil, k - 1)
                        for d in range(KD):
                            mm = pe.matmul(psum[0:f, k % 2, :], up_gate[y][0][:, d, c * P:c * P + f], hT[:, d, tok],
                                           start=(d == 0), stop=(d == KD - 1))
                        mm.then_inc(s_g, 1)
                        if k - K0[y] >= 2:
                            pe.wait_ge(s_hid, k - 1)
                        for d in range(KD):
                            mm = pe.matmul(psum[0:f, 2 + k % 2, :], up_gate[y][1][:, d, c * P:c * P + f], hT[:, d, tok],
                                           start=(d == 0), stop=(d == KD - 1))
                        if y == 1 and c < RC:
                            if tc == 0:
                                pe.wait_ge(s_le, 1)
                            pe.wait_ge(s_wt, NCH if tc == NCH - 1 else NCH - 1)
                            mm = pe.matmul(bank(4 + k % 2), esel[:, c, :], wT[0:3 * NE, tok], start=True, stop=True)
                        mm.then_inc(s_u, 1)
                    elif what == "down":
                        pe.wait_ge(s_hid, k)
                        pe.wait_ge(s_wd, y + 1)
                        for r in range(TPC):
                            j = y * NT + tc * TPC + r
                            if tc == 0 and r < 2:
                                pe.wait_ge(s_hte, 16 * (y + 1))
                                if y == 1:
                                    pe.wait_ge(s_le, 2)
                                    pe.wait_ge(s_wt, NCH)
                            else:
                                pe.wait_ge(s_xd, j - 1)
                            for cc in range(NC[y]):
                                f = fsize(y, cc)
                                mm = pe.matmul(bank(6 + j % 2)[:, 0:D], hid[tc % 2][0:f, cc, r * P:(r + 1) * P],
                                               down[0:f, cc, :], start=(cc == 0), stop=(cc == NC[y] - 1))
                            mm.then_inc(s_dn, 1)
                    elif what == "ln":
                        q = ln_of(y, tc, k)
                        for cc in range(KD):
                            ln(q, tc, cc)
                    elif what == "proj":
                        proj(1, tc)
                    elif what == "logits":
                        logits(tc)
                    elif what == "weights":
                        weights(tc)
                    elif c == 0:
                        sums_transpose(y, NU - 1)
                    elif c < 3:
                        back_transpose(y, NCH - 1, c - 1)
                    else:
                        output(y, NCH - 1, c - 3)

            for y in range(NLAY):
                if y == 0:
                    for tc in range(NCH):
                        for c in range(KD):
                            ln(0, tc, c)
                        if tc:
                            proj(0, tc - 1)
                    proj(0, NCH - 1)
                else:
                    pe.wait_ge(s_sil, K0[1])
                    pe.wait_ge(s_hid, K0[1])
                    pe.wait_ge(s_xd, NT)
                attention(y)
                pe.wait_ge(s_p, HG * S0[y + 1])
                ffn(y)

        @block.scalar
        def _(act):
            chain = [0]

            def link(ins):
                chain[0] += 1
                ins.then_inc(s_act, 1)
                act.wait_ge(s_act, chain[0])

            act.wait_ge(s_wmod, 48)
            nc.scalar.activation(ce[:, :], c_sb[:, :], ACT.Exp, scale=-1.0).then_inc(s_ce, 1)
            act.wait_ge(s_mod, NLAY)

            def ln(q, tc, c):
                y = q // 2
                if tc == 0 and c == 0 and q % 2:
                    act.wait_ge(s_vp, NT * (y + 1))
                if c == 0 and q == 2:
                    act.wait_ge(s_u, hid_end(0, tc))
                act.wait_ge(s_tr, 2 * (q * NCH + tc) + c + 1)
                i = 4 * (q % 2) + c
                nc.scalar.activation(hT[:, c, tc * CH:(tc + 1) * CH], bank(ln_bank(q, tc, c)), ACT.Identity,
                                     bias=modc[:, y, i:i + 1], scale=modc[:, y, i + 2:i + 3]).then_inc(s_hte, 1)

            def proj(y, tc):
                act.wait_ge(s_bs, y + 1)
                for side in range(2):
                    for f in range(KD):
                        k = (y * NCH + tc) * 4 + side * KD + f
                        b = k % 3
                        act.wait_ge(s_pj, k + 1)
                        if k >= 3:
                            act.wait_ge(s_l, k - 2)
                            act.wait_ge(s_split[b], 16 * (k // 3))
                        nc.scalar.activation(st_f[b], bank(2 + 2 * y + k % 2), ACT.Identity,
                                             bias=(b_row, b_col)[side][:, f:f + 1],
                                             scale=(1.0, SCALES[y])[side]).then_inc(s_qf, 1)
                        act.wait_ge(s_qf, k + 1)
                        nc.scalar.activation(st_p[b][:, 0, :], st_f[b], ACT.Identity).then_inc(s_h, 1)

            def attention(y):
                for s, n, k, _blocks in slot_walk(y):
                    if s >= 0:
                        i = n // NG
                        off = max(0, k - TPC * i) * P if CAUSAL[y] else 0
                        for h in range(HG):
                            e = HG * (S0[y] + s) + h
                            act.wait_ge(s_e, e + 1)
                            if S0[y] + s >= 2:
                                act.wait_ge(s_pv, S0[y] + s - 1)
                            nc.scalar.activation(probs[:, (S0[y] + s) % 2, h, off:CH], psum[:, e % 3, off:CH],
                                                 ACT.Exp).then_inc(s_p, 1)
                            if h == 1:
                                if k and back_slot(n, k - 1):
                                    copy_features(y, *back_slot(n, k - 1))
                                if k and ln_slot(n, k - 1):
                                    ln(2 * y + 1, *ln_slot(n, k - 1))
                                if k and mt_slot(y, n, k - 1) is not None:
                                    copy_maximum(y, mt_slot(y, n, k - 1))
                        if k == 0 and n > 0:
                            copy_out(y, n - 1)
                    else:
                        copy_maximum(y, 0)
                copy_out(y, NU - 1)

            def copy_maximum(y, m):
                act.wait_ge(s_mt, y * NU + m + 1)
                if y * NU + m:
                    act.wait_ge(s_mrow, 64 * (y * NU + m))
                nc.scalar.activation(mrow_t[:, :], bank(6 + m % 2), ACT.Identity).then_inc(s_mtc, 1)

            def copy_features(y, i, half_):
                act.wait_ge(s_bt, 2 * (y * NCH + i) + half_ + 1)
                if y * NCH + i and not half_:
                    act.wait_ge(s_op, 2 * (y * NCH + i))
                if i and not half_:
                    act.wait_ge(s_tr, 16 * y + 8 + 2 * i)
                nc.scalar.activation(attn_t[:, :, half_ * 2 * P:(half_ + 1) * 2 * P],
                                     bank(7).rearrange("p (k t) -> p k t", k=KD), ACT.Identity).then_inc(s_ac, 1)

            def copy_out(y, n):
                u = y * NU + n
                act.wait_ge(s_pv, unit_steps(y, n))
                if u:
                    act.wait_ge(s_ft, u)
                nc.scalar.activation(out_sb[:, :], bank(6 + n % 2), ACT.Identity).then_inc(s_oc, 1)

            def ffn(y):
                for what, tc, c, k in ffn_walk(y):
                    if what == "hid":
                        f = fsize(y, c)
                        act.wait_ge(s_g, k + 1)
                        if k >= 2:
                            act.wait_ge(s_hid, k - 1)
                        nc.scalar.activation(sil[k % 2][0:f, :], psum[0:f, k % 2, :], ACT.Silu,
                                             scale=gate_s[0:f, c:c + 1] if y == 0 else 1.0).then_inc(s_sil, 1)
                    elif what == "ln":
                        for cc in range(KD):
                            ln(ln_of(y, tc, k), tc, cc)
                    elif what == "proj":
                        proj(1, tc)
                    elif what == "logits":
                        lo, hi = ROUTE[tc]
                        act.wait_ge(s_lg, tc + 1)
                        nc.scalar.activation(r_s[:, lo:hi, :], bank(LB[tc])[:, lo * NE:hi * NE].rearrange("p (t e) -> p t e", e=NE),
                                             ACT.Exp, scale=-1.0).then_inc(s_le, 1)
                    elif what == "tail" and c in (1, 2):
                        copy_features(y, NCH - 1, c - 1)

            for y in range(NLAY):
                if y == 0:
                    for tc in range(NCH):
                        for c in range(KD):
                            ln(0, tc, c)
                        if tc:
                            proj(0, tc - 1)
                    proj(0, NCH - 1)
                attention(y)
                ffn(y)

        @block.vector
        def _(dve):
            chain = [0]

            def link(ins):
                chain[0] += 1
                ins.then_inc(s_dve, 1)
                dve.wait_ge(s_dve, chain[0])

            V = nc.vector
            link(V.memset(mp[:, :, :], 0.0))
            dve.wait_ge(s_ce, 1)
            link(V.tensor_scalar(ce[:, :], ce[:, :], 1.0, None, ALU.add))
            link(V.reciprocal(ce[:, :], ce[:, :]))
            link(V.tensor_tensor(cs[:, :], ce[:, :], c_sb[:, :], ALU.mult))
            for k in range(2 * KD):
                ins = V.tensor_copy(csb[:, k, :], cs[:, k:k + 1].to_broadcast([P, P]))
            ins.then_inc(s_cs, 1)
            for y in range(NLAY):
                dve.wait_ge(s_modp, y + 1)
                g = gab[:, y, :]
                link(V.tensor_copy(g, bank(2 * y)))
                link(V.tensor_copy(modc[:, y, :], bank(2 * y + 1)[:, 0:8]))
                for i in (2, 6):
                    link(V.tensor_scalar(modc[:, y, i:i + 2], modc[:, y, i:i + 2], 1.0, None, ALU.add))
                link(V.tensor_scalar(gtmp[:, 0, :], g, 0.0, 2.0, ALU.is_ge, ALU.mult))
                link(V.scalar_tensor_tensor(gtmp[:, 1, :], g, -1.0, g, ALU.mult, ALU.max))
                link(V.tensor_scalar(gtmp[:, 1, :], gtmp[:, 1, :], 0.25, None, ALU.max))
                ins = V.scalar_tensor_tensor(g, gtmp[:, 0, :], -1.0, gtmp[:, 1, :], ALU.add, ALU.mult)
                if y == 0:
                    link(ins)
                    dve.wait_ge(s_const, 160)
                    ins = V.tensor_tensor(g[:, D:2 * D], g[:, D:2 * D], down_s[:, :], ALU.mult)
                ins.then_inc(s_mod, 1)

            def stats_of(q, tc):
                if q == 0:
                    dve.wait_ge(s_x, 16 * NCH)
                elif q % 2 == 1:
                    dve.wait_ge(s_xa, 8 * (q // 2) + 2 * (tc + 1))
                else:
                    dve.wait_ge(s_xd, TPC * (tc + 1))
                j = q * NCH + tc
                for t in range(TPC):
                    ins = V.bn_stats(stats[:, t, :], x_sb[:, tc * TPC + t, :])
                link(ins)
                if j >= 2:
                    dve.wait_ge(s_xh, j - 1)
                    dve.wait_ge(s_rstd, j - 1)
                for t in range(TPC):
                    ins = V.bn_aggr(mv[:, tc % 2, t, :], stats[:, t, :])
                ins.then_inc(s_mv, 1)
                dve.wait_ge(s_mv, j + 1)

            def normed(q, tc):
                j = q * NCH + tc
                dve.wait_ge(s_rstd, j + 1)
                if j >= 2:
                    dve.wait_ge(s_tr, 2 * (j if q % 2 else j - 1))
                for t in range(TPC):
                    ins = V.tensor_scalar(xh[:, xh_buf(q, tc), t, :], x_sb[:, tc * TPC + t, :], mv[:, tc % 2, t, 0:1],
                                          rstd[:, tc % 2, t:t + 1], ALU.subtract, ALU.mult)
                ins.then_inc(s_xh, 1)

            def scale_bias(y):
                dve.wait_ge(s_wattn, 128 * (y + 1))
                if y:
                    dve.wait_ge(s_qf, 16)
                V.tensor_scalar(b_col[:, :], b_colr[:, :], SCALES[y], None, ALU.mult).then_inc(s_bs, 1)

            def split(y, tc):
                for k in range(4 * (y * NCH + tc), 4 * (y * NCH + tc) + 4):
                    b = k % 3
                    dve.wait_ge(s_h, k + 1)
                    link(V.tensor_tensor(st_r[b], st_f[b], st_p[b][:, 0, :], ALU.subtract))
                    link(V.tensor_copy(st_p[b][:, 1, :], st_r[b]))
                    V.tensor_tensor(st_p[b][:, 2, :], st_r[b], st_p[b][:, 1, :], ALU.subtract).then_inc(s_l, 1)

            def ones(y):
                if y == 1:
                    dve.wait_ge(s_dn, NT)
                link(V.memset(v_sb[:, :, :, HD], 1.0))

            def value(y, t):
                v = y * NT + t
                dve.wait_ge(s_vp, v + 1)
                V.tensor_tensor(v_sb[:, t, :, 0:HD], bank(6 + v % 2)[:, 0:D].rearrange("p (h c) -> p h c", h=H),
                                b_v[:, :].rearrange("p (h c) -> p h c", h=H), ALU.add).then_inc(s_ve, 1)

            def normalise(y, n):
                u, g = y * NU + n, n % NG
                if g == 0 and n > 0:
                    dve.wait_ge(s_bt, 2 * (y * NCH + n // NG))
                dve.wait_ge(s_ft, u + 1)
                if u:
                    dve.wait_ge(s_on, u)
                sums = bank(6 + n % 2).rearrange("p (t h c) -> p t h c", t=TPC, h=HG)
                link(V.reciprocal(rden[:, :, :], sums[:, :, :, HD]))
                V.tensor_tensor(attn_n[:, :, g * GF:(g + 1) * GF].rearrange("p t (h c) -> p t h c", h=HG),
                                sums[:, :, :, 0:HD], rden[:, :, :].unsqueeze(3).to_broadcast([P, TPC, HG, HD]),
                                ALU.mult).then_inc(s_on, 1)

            def add_output(y, i, half_):
                j = 8 * y + 2 * i + half_
                dve.wait_ge(s_obg, y + 1)
                dve.wait_ge(s_op, j + 1)
                t = TPC * i + 2 * half_
                V.tensor_tensor(x_sb[:, t:t + 2, :], bank(7).rearrange("p (t d) -> p t d", t=2), x_sb[:, t:t + 2, :],
                                ALU.add).then_inc(s_xa, 1)

            def attention(y):
                mb = [M0[y]]

                def reduce_block(n, h, r, q):
                    b = mb[0]
                    mb[0] += 1
                    chunks = n // NG + 1 if CAUSAL[y] else NCH
                    last = CAUSAL[y] and q == n // NG
                    w = (r + 1) * P if last else CH
                    dve.wait_ge(s_mb, b + 1)
                    V.tensor_reduce(mpart[:, h * TPC + r, q:q + 1], bank(3 + b % 3)[:, 0:w], AX.X, ALU.max).then_inc(s_mr, 1)
                    if (h, r, q) == (HG - 1, TPC - 1, chunks - 1):
                        dve.wait_ge(s_mr, b + 1)
                        u = y * NU + n
                        link(V.tensor_reduce(mx[:, :], mpart[:, :, 0:chunks], AX.X, ALU.max))
                        link(V.tensor_scalar(mx[:, :], mx[:, :], ROUND, -ROUND, ALU.add, ALU.add))
                        if u:
                            dve.wait_ge(s_mt, u)
                        link(V.tensor_scalar(mp[:, :, 0], mx[:, :], -1.0, None, ALU.mult))
                        V.scalar_tensor_tensor(mp[:, :, 1], mx[:, :], -1.0, mp[:, :, 0], ALU.mult, ALU.subtract).then_inc(s_mp, 1)

                first = plans[y][0]
                for t in range(NT // 2):
                    value(y, t)
                for m, b in enumerate(first):
                    reduce_block(*b)
                    if (m + 1) % (len(first) // (NT // 2)) == 0:
                        value(y, NT // 2 + (m + 1) // (len(first) // (NT // 2)) - 1)
                for s, n, k, blocks in slot_walk(y):
                    if s >= 0 and k == 2 and n > 0:
                        normalise(y, n - 1)
                    if s >= 0 and k and oproj_slot(n, k - 1):
                        add_output(y, *oproj_slot(n, k - 1))
                        if oproj_slot(n, k - 1)[1]:
                            stats_of(2 * y + 1, n // NG - 1)
                    for b in blocks:
                        reduce_block(*b)
                    if s >= 0 and n % NG == 0 and n > 0 and k == 7:
                        normed(2 * y + 1, n // NG - 1)

            def router(part):
                dve.wait_ge(s_le, part + 1)
                lo, hi = ROUTE[part]
                n = hi - lo
                ts = slice(lo, hi)
                link(V.tensor_scalar(r_s[:, ts, :], r_s[:, ts, :], 1.0, None, ALU.add))
                link(V.reciprocal(r_s[:, ts, :], r_s[:, ts, :]))
                mine = r_s[:, ts, :].unsqueeze(3).to_broadcast([P, n, NE, NE])
                other = r_s[:, ts, :].unsqueeze(2).to_broadcast([P, n, NE, NE])
                low = tri[:, :, :].unsqueeze(1).to_broadcast([P, n, NE, NE])
                link(V.tensor_tensor(r_gt[:, ts, :, :], other, mine, ALU.is_gt))
                link(V.tensor_tensor(r_eq[:, ts, :, :], other, mine, ALU.is_equal))
                link(V.tensor_tensor(r_eq[:, ts, :, :], r_eq[:, ts, :, :], low, ALU.mult))
                link(V.tensor_tensor(r_gt[:, ts, :, :], r_gt[:, ts, :, :], r_eq[:, ts, :, :], ALU.add))
                link(V.tensor_reduce(r_rank[:, ts, :], r_gt[:, ts, :, :], AX.X, ALU.add))
                link(V.tensor_scalar(r_rank[:, ts, :], r_rank[:, ts, :], 2.0, None, ALU.is_lt))
                link(V.tensor_tensor(r_w[:, ts, :], r_rank[:, ts, :], r_s[:, ts, :], ALU.mult))
                link(V.tensor_reduce(r_sum[:, ts], r_w[:, ts, :], AX.X, ALU.add))
                link(V.tensor_scalar(r_sum[:, ts], r_sum[:, ts], 1e-20, None, ALU.add))
                link(V.reciprocal(r_inv[:, ts], r_sum[:, ts]))
                link(V.tensor_scalar(r_inv[:, ts], r_inv[:, ts], 2.5, None, ALU.mult))
                link(V.tensor_tensor(r_w[:, ts, :], r_w[:, ts, :], r_inv[:, ts].unsqueeze(2).to_broadcast([P, n, NE]), ALU.mult))
                link(V.tensor_copy(r_p[:, ts, 0, :], r_w[:, ts, :]))
                link(V.tensor_tensor(r_lo[:, ts, :], r_w[:, ts, :], r_p[:, ts, 0, :], ALU.subtract))
                link(V.tensor_copy(r_p[:, ts, 1, :], r_lo[:, ts, :]))
                V.tensor_tensor(r_p[:, ts, 2, :], r_lo[:, ts, :], r_p[:, ts, 1, :], ALU.subtract).then_inc(s_rp, 1)

            def weights(part):
                for tc in range(ROUTE[part][0] // TPC, ROUTE[part][1] // TPC):
                    dve.wait_ge(s_rt, tc + 1)
                    V.tensor_copy(wT[0:3 * NE, tc * CH:(tc + 1) * CH], psum[0:3 * NE, WB[part], :]).then_inc(s_wt, 1)

            def ffn(y):
                first_hid = {}
                for what, tc, c, k in ffn_walk(y):
                    if what == "hid":
                        f = fsize(y, c)
                        dve.wait_ge(s_sil, k + 1)
                        dve.wait_ge(s_u, k + 1)
                        if first_hid.setdefault(tc, k) == k and tc >= 2:
                            dve.wait_ge(s_dn, y * NT + (tc - 1) * TPC)
                        dst, up = hid[tc % 2][0:f, c, :], psum[0:f, 2 + k % 2, :]
                        if y == 0:
                            V.scalar_tensor_tensor(dst, up, up_s[0:f, c:c + 1], sil[k % 2][0:f, :], ALU.mult, ALU.mult).then_inc(s_hid, 1)
                        elif c < RC:
                            link(V.tensor_tensor(utmp[k % 2], up, sil[k % 2], ALU.mult))
                            V.tensor_tensor(dst, bank(4 + k % 2), utmp[k % 2], ALU.mult).then_inc(s_hid, 1)
                        else:
                            V.tensor_tensor(dst, up, sil[k % 2][0:f, :], ALU.mult).then_inc(s_hid, 1)
                    elif what == "down":
                        for r in range(TPC):
                            j = y * NT + tc * TPC + r
                            dve.wait_ge(s_dn, j + 1)
                            t = tc * TPC + r
                            V.tensor_tensor(x_sb[:, t, :], bank(6 + j % 2)[:, 0:D], x_sb[:, t, :], ALU.add).then_inc(s_xd, 1)
                        if y == 0:
                            stats_of(2, tc)
                            normed(2, tc)
                    elif what == "proj":
                        split(1, tc)
                    elif what == "logits":
                        router(tc)
                    elif what == "weights":
                        weights(tc)
                    elif what == "ln" and y == 0 and ln_of(y, tc, k) == 1:
                        scale_bias(1)
                    elif what == "tail" and c == 0:
                        normalise(y, NU - 1)
                    elif what == "tail" and c == 3:
                        add_output(y, NCH - 1, 0)
                    elif what == "tail" and c == 4:
                        add_output(y, NCH - 1, 1)
                        stats_of(2 * y + 1, NCH - 1)
                        normed(2 * y + 1, NCH - 1)

            scale_bias(0)
            ones(0)
            stats_of(0, 0)
            for tc in range(NCH):
                if tc + 1 < NCH:
                    stats_of(0, tc + 1)
                normed(0, tc)
                if tc:
                    split(0, tc - 1)
            split(0, NCH - 1)
            for y in range(NLAY):
                attention(y)
                ffn(y)
                if y == 0:
                    ones(1)


def constants():
    bf = np.dtype("bfloat16")
    t = np.arange(T)
    i = np.arange(P)
    col = np.ones((CR, HG, T), np.float32)
    col[2], col[4] = t // 256 * 256, t % 256
    row0 = np.zeros((CR, HG, T), np.float32)
    row0[2], row0[3], row0[4], row0[5] = 1, -(t // 256 * 256), 1, -(t % 256)
    e = np.arange(NE)
    esel = np.zeros((3 * NE, RC, P), np.float32)
    for f in range(NE * FE):
        esel[f // FE::NE, f // P, f % P] = 1
    return {
        "ident": np.eye(P, dtype=np.float32), "identb": np.eye(P).astype(bf),
        "neg_m": np.where(i[None, :] > i[:, None], -1e30, 0).astype(bf),
        "neg_e": np.where(i[:, None] > i[None, :], -1e30, 0).astype(bf),
        "col_const": col.astype(bf), "row_const0": row0.astype(bf), "row_const1": np.zeros((CR, HG, T), bf),
        "tri": (e[None, :] < e[:, None]).astype(np.float32), "esel": esel.astype(bf),
    }


def laid_out(v):
    v = {k: np.asarray(x) for k, x in v.items()}

    def columns(b):
        n = -(-b.shape[0] // P)
        out = np.zeros((n * P,), b.dtype)
        out[:b.shape[0]] = b
        return np.ascontiguousarray(out.reshape(n, P).T)

    c = np.concatenate([v["L0_c"].reshape(KD, P), v["L1_c"].reshape(KD, P)]).T
    a = {
        "x": v["L0_attn_x"].reshape(T, D), "c": c, "wmod0": v["L0_wmod"], "wmod1": v["L1_wmod"],
        "w_row0": v["L0_attn_k_w"].T, "w_col0": v["L0_attn_q_w"].T, "w_v0": v["L0_attn_v_w"].T,
        "b_row0": columns(v["L0_attn_k_b"]), "b_col0": columns(v["L0_attn_q_b"]),
        "b_v0": v["L0_attn_v_b"], "b_o0": v["L0_attn_o_b"], "w_o0": v["L0_attn_o_w"].T,
        "w_row1": v["L1_attn_wq"], "w_col1": v["L1_attn_wk"], "w_v1": v["L1_attn_wv"],
        "b_row1": columns(v["L1_attn_bq"]), "b_col1": columns(v["L1_attn_bk"]),
        "b_v1": v["L1_attn_bv"], "b_o1": v["L1_attn_bo"], "w_o1": v["L1_attn_wo"],
        "w_gate0": v["L0_ffn_gate_w"].T, "w_up0": v["L0_ffn_up_w"].T, "w_down0": v["L0_ffn_down_w"].T,
        "gate_s": columns(v["L0_ffn_gate_s"]), "up_s": columns(v["L0_ffn_up_s"]), "down_s": v["L0_ffn_down_s"],
        "w_gate1": np.concatenate([v["L1_ffn_exp_wg"].reshape(NE * FE, D), v["L1_ffn_shared_wg"]]).T,
        "w_up1": np.concatenate([v["L1_ffn_exp_wu"].reshape(NE * FE, D), v["L1_ffn_shared_wu"]]).T,
        "w_down1": np.concatenate([v["L1_ffn_exp_wd"].transpose(0, 2, 1).reshape(NE * FE, D), v["L1_ffn_shared_wd"].T]),
        "gate_w": v["L1_ffn_gate_w"].T,
    }
    return {k: np.ascontiguousarray(x) for k, x in {**a, **constants()}.items()}


def kernel(**inputs):
    import concourse.bacc as bacc
    from concourse.bass_utils import run_bass_kernel_spmd

    arrays = laid_out(inputs)
    nc = bacc.Bacc("TRN2", target_bir_lowering=False, num_devices=1)
    aps = {k: nc.dram_tensor(f"in_{k}", x.shape, mybir.dt.from_np(x.dtype), kind="ExternalInput").ap()
           for k, x in arrays.items()}
    aps["out"] = nc.dram_tensor("out", (T, D), F32, kind="ExternalOutput").ap()
    adaln_two_layers(nc, aps)
    got = run_bass_kernel_spmd(nc, [{f"in_{k}": x for k, x in arrays.items()}], core_ids=[0])
    return got.results[0]["out"].reshape(1, T, D)
```

```python
from contextlib import ExitStack

import numpy as np
import concourse.bass as bass
from concourse import mybir

F32 = mybir.dt.float32
BF16 = mybir.dt.bfloat16
ALU = mybir.AluOpType
ACT = mybir.ActivationFunctionType
AX = mybir.AxisListType

P = 128
T = 2048
D = 256
KD = D // P
NT = T // P
CH = 512
NCH = T // CH
TPC = CH // P
H = 16
HD = D // H
HG = 4
NG = H // HG
GF = HG * HD
VW = HD + 1
SLOTS_ROW = (0, 0, 1, 1, 0, 2)
SLOTS_COL = (0, 1, 0, 1, 2, 0)
CR = 6
KS = CR + HD * len(SLOTS_ROW)
SCALES = (HD ** -0.5, D ** -0.5)
ROUND = 12582912.0
EPS = 1e-5
NE = 8
FE = 176
F0 = 704
F1 = NE * FE + 2 * FE
FS = (F0, F1)
NC = tuple(-(-f // P) for f in FS)
RC = NE * FE // P
ROUTE = ((0, 3 * NT // 4), (3 * NT // 4, NT))
LB, WB = (4, 6), (5, 7)
CAUSAL = (True, False)
NLAY = 2
EARLY = {(2, 2): (2, 2), (2, 3): (2, 0), (3, 0): (2, 2), (3, 1): (2, 2), (3, 2): (2, 2), (3, 3): (2, 0), (3, 5): (0, 2)}
EARLY_DOWN = 2
NEARLY = sum(map(sum, EARLY.values())) + TPC * EARLY_DOWN


def fsize(layer, c):
    return min(P, FS[layer] - P * c)


def steps_of(layer, n):
    return TPC * (n // NG + 1) if CAUSAL[layer] else NT


def plan(layer):
    units = NCH * NG
    blocks, ends = [], []
    for n in range(units):
        chunks = n // NG + 1 if CAUSAL[layer] else NCH
        blocks += [(n, h, r, q) for h in range(HG) for r in range(TPC) for q in range(chunks)]
        if n == 0:
            blocks.sort(key=lambda b: b[3])
        ends.append(len(blocks))
    start = [sum(steps_of(layer, m) for m in range(n)) for n in range(units)]
    total = start[-1] + steps_of(layer, units - 1)
    slots, done = [], ends[0]
    first = blocks[:done]
    for s in range(-1, total):
        want = len(blocks)
        for n in range(1, units):
            a, b = start[n - 1] - 4, start[n] - 4
            if a <= s < b:
                want = ends[n - 1] + (ends[n] - ends[n - 1]) * (s - a) // (b - a)
        want = max(want, done)
        slots.append(blocks[done:want])
        done = want
    return first, slots, start, total


def adaln_two_layers(nc, a):
    ctx = ExitStack()
    with ctx:
        def sb(name, shape, dt=F32):
            return ctx.enter_context(nc.sbuf_tensor(name, shape, dt))

        def sem(name):
            return ctx.enter_context(nc.semaphore(name))

        x_sb = sb("x_sb", [P, NT, D])
        key_region = sb("key_region", [P, H * T // 2])
        v_region = sb("v_region", [P, NT * H * VW])
        row_region = sb("row_region", [P, NG * HG * CH // 2])
        probs = sb("probs", [P, 2, HG, CH])
        hT = sb("hT", [P, KD, T])
        attn_region = sb("attn_region", [P, 2 * KD * CH])
        ffn_w = sb("ffn_w", [P, 2, KD * F1])
        w_row = sb("w_row", [P, KD, D])
        w_col = sb("w_col", [P, KD, D])
        w_v = sb("w_v", [P, KD, D])
        w_o = sb("w_o", [P, KD, D])
        b_row = sb("b_row", [P, KD])
        b_col = sb("b_col", [P, KD])
        b_colr = sb("b_colr", [P, KD])
        b_v = sb("b_v", [P, D])
        b_o = sb("b_o", [P, D])
        out_sb = sb("out_sb", [P, CH])
        rden = sb("rden", [P, TPC, HG])
        mrow_t = sb("mrow_t", [P, CH], BF16)
        mpart = sb("mpart", [P, HG * TPC, NCH])
        mx = sb("mx", [P, HG * TPC])
        mp = sb("mp", [P, HG * TPC, 32], BF16)
        ident = sb("ident", [P, P])
        identb = sb("identb", [P, P], BF16)
        neg_m = sb("neg_m", [P, P], BF16)
        neg_e = sb("neg_e", [P, P], BF16)
        gab = sb("gab", [P, NLAY, 2 * D])
        modc = sb("modc", [P, NLAY, 8])
        stats = sb("stats", [P, TPC, 6])
        mv = sb("mv", [P, 2, TPC, 2])
        rstd = sb("rstd", [P, 2, TPC])
        vare = sb("vare", [P, TPC])
        half = sb("half", [P, TPC])
        c_sb = sb("c_sb", [P, 2 * KD])
        ce = sb("ce", [P, 2 * KD])
        cs = sb("cs", [P, 2 * KD])
        gate_s = sb("gate_s", [P, NC[0]])
        up_s = sb("up_s", [P, NC[0]])
        down_s = sb("down_s", [P, D])
        gate_w = sb("gate_w", [P, KD, NE])
        tri = sb("tri", [P, NE, NE])
        esel = sb("esel", [3 * NE, RC, P], BF16)

        keys = key_region[:, :].bitcast(BF16).rearrange("p (h t) -> p h t", h=H)
        v_sb = v_region[:, :].rearrange("p (t h c) -> p t h c", t=NT, h=H)
        rows = row_region[:, :].bitcast(BF16).rearrange("p (g h t) -> p g h t", g=NG, h=HG)
        attn_n = attn_region[:, 0:TPC * D].rearrange("p (t d) -> p t d", t=TPC)
        attn_t = attn_region[:, TPC * D:].rearrange("p (k t) -> p k t", k=KD)
        WM = KD * 6 * D
        wmod = [key_region[:, y * WM:(y + 1) * WM].rearrange("p (k n) -> p k n", k=KD) for y in range(NLAY)]
        o1 = NLAY * WM
        csb = key_region[:, o1:o1 + 2 * KD * P].rearrange("p (k n) -> p k n", k=2 * KD)
        o1 += 2 * KD * P
        gtmp = key_region[:, o1:o1 + 3 * 2 * D].rearrange("p (k n) -> p k n", k=3)
        SW = CH * 2 + 3 * CH // 2
        KG = HG * T // 2
        o2 = KG + 2 * NC[0] * CH
        stage = [key_region[:, o2 + b * SW:o2 + (b + 1) * SW] for b in range(3)]
        st_f = [s[:, 0:CH] for s in stage]
        st_r = [s[:, CH:2 * CH] for s in stage]
        st_p = [s[:, 2 * CH:SW].bitcast(BF16).rearrange("p (k t) -> p k t", k=3) for s in stage]
        xh = attn_region[:, :].rearrange("p (b t d) -> p b t d", b=2, t=TPC)
        hid = [[key_region[:, o + b * n * CH:o + (b + 1) * n * CH].rearrange("p (c t) -> p c t", c=n) for b in range(2)]
               for o, n in zip((KG, 0), NC)]
        sil = [probs[:, 0, b, :] for b in range(2)]
        utmp = [probs[:, 0, 2 + b, :] for b in range(2)]
        down = v_region[:, 0:NC[1] * D].rearrange("p (c d) -> p c d", c=NC[1])
        up_gate = [[ffn_w[:, i, 0:KD * FS[y]].rearrange("p (k f) -> p k f", k=KD) for i in range(2)]
                   for y in range(NLAY)]
        ro = [0]

        def take(n):
            ro[0] += n
            return row_region[:, ro[0] - n:ro[0]]

        r_s = take(NT * NE).rearrange("p (t e) -> p t e", t=NT)
        r_gt = take(NT * NE * NE).rearrange("p (t e f) -> p t e f", t=NT, e=NE)
        r_eq = take(NT * NE * NE).rearrange("p (t e f) -> p t e f", t=NT, e=NE)
        r_rank = take(NT * NE).rearrange("p (t e) -> p t e", t=NT)
        r_w = take(NT * NE).rearrange("p (t e) -> p t e", t=NT)
        r_sum = take(NT)
        r_inv = take(NT)
        r_lo = take(NT * NE).rearrange("p (t e) -> p t e", t=NT)
        r_p = take(NT * 3 * NE // 2).bitcast(BF16).rearrange("p (t k e) -> p t k e", t=NT, k=3)
        wT = take(T // 2).bitcast(BF16)

        psum = ctx.enter_context(nc.psum_tensor("psum", [P, 8, CH], F32))

        def bank(b):
            return psum[:, b, :]

        parts = nc.dram_tensor("parts", (2, 3, D, T), BF16, kind="Internal").ap()

        s_x = [sem(f"x_loaded{tc}") for tc in range(NCH)]
        s_c = sem("c_loaded")
        s_ident = sem("identity_loaded")
        s_const = sem("constants_loaded")
        s_wmod = [sem(f"modulation_weights_loaded{y}") for y in range(NLAY)]
        s_wattn = sem("attention_weights_loaded")
        s_wffn = sem("ffn_weights_loaded")
        s_wdown = sem("down_weights_loaded")
        s_dve = sem("vector_chain")
        s_act = sem("scalar_chain")
        s_pool = sem("gpsimd_chain")
        s_ce = sem("exp_c_done")
        s_cs = sem("silu_c_spread")
        s_modp = sem("modulation_product")
        s_modc = sem("shifts_and_scales_ready")
        s_mod = sem("gates_ready")
        s_wo = sem("output_weights_scaled")
        s_wd = sem("down_weights_scaled")
        s_obg = sem("output_bias_added")
        s_mv = sem("ln_stats_ready")
        s_rstd = sem("ln_rstd_ready")
        s_xh = sem("normed_ready")
        s_tr = sem("normed_transposed")
        s_hte = sem("h_ready")
        s_pj = sem("projection_product")
        s_qf = sem("projection_evacuated")
        s_bs = sem("column_bias_scaled")
        s_h = sem("high_part_ready")
        s_l = sem("low_part_ready")
        s_split = [sem(f"parts_stored{b}") for b in range(3)]
        s_vp = sem("value_product")
        s_ve = sem("values_ready")
        s_key = [sem(f"keys_loaded{g}") for g in range(NG)]
        s_chunk = [sem(f"chunk_of_first_keys_loaded{q}") for q in range(NCH)]
        s_row = [sem(f"rows_loaded{g}") for g in range(NG)]
        s_mb = sem("max_block_product")
        s_mr = sem("max_block_reduced")
        s_mp = sem("max_parts_ready")
        s_mt = sem("max_transposed")
        s_mtc = sem("max_rows_copied")
        s_mrow = sem("max_rows_placed")
        s_e = sem("scores_ready")
        s_p = sem("probs_ready")
        s_pv = sem("probs_used")
        s_oc = sem("attn_copied")
        s_ft = sem("sums_transposed")
        s_on = sem("attn_normalised")
        s_bt = sem("attn_transposed")
        s_ac = sem("attn_features_copied")
        s_op = sem("output_product")
        s_xa = sem("attn_added")
        s_g = sem("gate_product")
        s_u = sem("up_product")
        s_sil = sem("silu_ready")
        s_hid = sem("hidden_ready")
        s_dn = sem("down_product")
        s_xd = sem("ffn_added")
        s_lg = sem("router_product")
        s_le = sem("router_exp")
        s_rp = sem("router_parts_ready")
        s_rt = sem("router_transposed")
        s_wt = sem("router_rows_ready")
        s_out = sem("output_stored")

        plans = [plan(y) for y in range(NLAY)]
        STEPS = [p[3] for p in plans]
        S0 = [0, STEPS[0], STEPS[0] + STEPS[1]]
        MB = [sum(len(s) for s in p[1]) + len(p[0]) for p in plans]
        M0 = [0, MB[0], MB[0] + MB[1]]
        NU = NCH * NG
        K0 = [0, NC[0] * NCH, (NC[0] + NC[1]) * NCH]
        EARLY0, EARLY1 = M0[1], M0[1] + NEARLY

        def mb_bank(b):
            return 4 + b % 2 if EARLY0 <= b < EARLY1 else 3 + b % 3

        def score_bank(n, e):
            return e % 6 if n == NU - 1 else e % 3

        def prologue(y):
            first = plans[y][0][NEARLY if y else 0:]
            if y:
                seq = [w for m in range(NT) for w in (("value", m), ("block", first[m]))]
                return seq + [("block", b) for b in first[NT:]]
            seq = [("value", t) for t in range(3 * NT // 4)]
            for m, b in enumerate(first):
                seq.append(("block", b))
                if m % 4 == 3:
                    seq.append(("value", 3 * NT // 4 + m // 4))
            return seq

        def slot_walk(y):
            first, slots, start, total = plans[y]
            for s in range(-1, total):
                n = max(m for m in range(NU) if start[m] <= max(s, 0))
                yield s, n, s - start[n], slots[s + 1]

        def unit_steps(y, n):
            return S0[y] + plans[y][2][n] + steps_of(y, n)

        def mt_slot(y, n, k):
            return n + 1 if n + 1 < NU and k == steps_of(y, n) - 3 else None

        def oproj_slot(n, k):
            return (n // NG - 1, k - 4) if n % NG == 0 and n > 0 and k in (4, 5) else None

        def back_slot(n, k):
            return (n // NG - 1, k - 2) if n % NG == 0 and n > 0 and k in (2, 3) else None

        def ln_slot(n, k):
            return (n // NG - 1, k - 2) if n % NG == 1 and n > 1 and k in (2, 3) else None

        def ln_bank(q, tc, c):
            if q == 0:
                return c
            if q == 2:
                return 4 + c
            return 6 if tc < NCH - 1 else 6 + c

        def ffn_walk(y):
            seq = []
            if y == 0:
                for tc in range(NCH):
                    for c in range(NC[0]):
                        seq.append(("hid", tc, c))
                        if tc == 0 and c < 5:
                            seq.append(("tail", 0, c))
                        if (tc, c) == (1, 0):
                            seq.append(("ln", NCH - 1, 0))
                        if tc > 0 and c in (1, 3, 4):
                            seq.append(({1: "down", 3: "ln", 4: "proj"}[c], tc - 1, 0))
                seq += [(w, NCH - 1, 0) for w in ("down", "ln", "proj")]
            else:
                shared, routed = list(range(RC, NC[1])), list(range(RC))
                seq.append(("logits", 0, 0))
                for m, (tc, c) in enumerate([(tc, c) for tc in range(2) for c in shared]):
                    seq.append(("hid", tc, c))
                    if m == 2:
                        seq.append(("weights", 0, 0))
                    if m < 5:
                        seq.append(("tail", 0, m))
                seq += [("hid", 0, c) for c in routed[:1]] + [("ln", NCH - 1, 0)]
                seq += [("hid", 0, c) for c in routed[1:3]] + [("logits", 1, 0)]
                seq += [("hid", 0, c) for c in routed[3:7]] + [("weights", 1, 0)]
                seq += [("hid", 0, c) for c in routed[7:]]
                seq += [("hid", 1, c) for c in routed[:2]] + [("down", 0, 0)] + [("hid", 1, c) for c in routed[2:]]
                for tc in range(2, NCH):
                    order = shared + routed
                    seq += [("hid", tc, c) for c in order[:2]] + [("down", tc - 1, 0)] + [("hid", tc, c) for c in order[2:]]
                seq.append(("down", NCH - 1, 0))
            done = K0[y]
            last = {}
            for what, tc, c in seq:
                if what == "hid":
                    last[tc] = done + 1
                    yield what, tc, c, done
                    done += 1
                else:
                    yield what, tc, c, last.get(tc, done) if what == "down" else done

        def ln_of(y, tc, k):
            return 2 * y + 1 if y or tc == NCH - 1 and k <= K0[y] + NC[0] + 1 else 2

        def xh_buf(q, tc):
            return 1 if q % 2 else tc % 2

        def hid_end(y, tc):
            return max(k + 1 for what, t, _c, k in ffn_walk(y) if what == "hid" and t == tc)

        block = ctx.enter_context(nc.Block())

        @block.sync
        def _(sp):
            def load_attn(y):
                for dst, name in ((w_row, "w_row"), (w_col, "w_col"), (w_v, "w_v")):
                    sp.dma_start(dst[:, :, :], a[f"{name}{y}"].rearrange("(k p) n -> p k n", p=P)).then_inc(s_wattn, 16)
                sp.dma_start(w_o[:, :, :], a[f"w_o{y}"].rearrange("(k p) n -> p k n", p=P)).then_inc(s_wattn, 16)
                sp.dma_start(b_row[:, :], a[f"b_row{y}"]).then_inc(s_wattn, 16)
                sp.dma_start(b_colr[:, :], a[f"b_col{y}"]).then_inc(s_wattn, 16)
                sp.dma_start(b_v[:, :], a[f"b_v{y}"].partition_broadcast(P)).then_inc(s_wattn, 16)
                sp.dma_start(b_o[:, :], a[f"b_o{y}"].partition_broadcast(P)).then_inc(s_wattn, 16)

            def load_ffn(y):
                for i, name in enumerate(("w_gate", "w_up")):
                    sp.dma_start(up_gate[y][i], a[f"{name}{y}"].rearrange("(k p) n -> p k n", p=P)).then_inc(s_wffn, 16)

            def load_down(y):
                full = FS[y] // P
                sp.dma_start(down[:, 0:full, :], a[f"w_down{y}"][0:full * P, :].rearrange("(c p) d -> p c d", p=P)).then_inc(s_wdown, 16)
                sp.dma_start(down[0:FS[y] - full * P, full, :], a[f"w_down{y}"][full * P:FS[y], :]).then_inc(s_wdown, 16)

            def load_rows(y, n):
                i, g = n // NG, n % NG
                if n >= NG:
                    sp.wait_ge(s_e, HG * unit_steps(y, n - NG))
                sp.dma_start(rows[0:CR, g, :, :], a[f"row_const{y}"][:, :, i * CH:(i + 1) * CH]).then_inc(s_row[g], 16)
                for k, part in enumerate(SLOTS_ROW):
                    src = parts[0, part, g * GF:(g + 1) * GF, i * CH:(i + 1) * CH].rearrange("(h c) t -> c h t", c=HD)
                    sp.dma_start(rows[CR + HD * k:CR + HD * (k + 1), g, :, :], src).then_inc(s_row[g], 16)

            def place_maximum(y, m):
                sp.wait_ge(s_mtc, y * NU + m + 1)
                for h in range(HG):
                    sp.dma_start(rows[0:2, m % NG, h, :], mrow_t[32 * h:32 * h + 2, :]).then_inc(s_mrow, 16)

            def load_key_chunk(q):
                tok = slice(q * CH, (q + 1) * CH)
                sp.dma_start(keys[0:CR, 0:HG, tok], a["col_const"][:, :, tok]).then_inc(s_chunk[q], 16)
                for k, part in enumerate(SLOTS_COL):
                    src = parts[1, part, 0:GF, tok].rearrange("(h c) t -> c h t", c=HD)
                    sp.dma_start(keys[CR + HD * k:CR + HD * (k + 1), 0:HG, tok], src).then_inc(s_chunk[q], 16)

            def load_keys(g):
                sp.dma_start(keys[0:CR, g * HG:(g + 1) * HG, :], a["col_const"]).then_inc(s_key[g], 16)
                for k, part in enumerate(SLOTS_COL):
                    src = parts[1, part, g * GF:(g + 1) * GF, :].rearrange("(h c) t -> c h t", c=HD)
                    sp.dma_start(keys[CR + HD * k:CR + HD * (k + 1), g * HG:(g + 1) * HG, :], src).then_inc(s_key[g], 16)

            def load_x(tc):
                sp.dma_start(x_sb[:, tc * TPC:(tc + 1) * TPC, :],
                             a["x"][tc * CH:(tc + 1) * CH, :].rearrange("(t p) d -> p t d", p=P)).then_inc(s_x[tc], 16)

            def load_wmod(y):
                sp.dma_start(wmod[y], a[f"wmod{y}"].rearrange("(k p) n -> p k n", p=P)).then_inc(s_wmod[y], 16)

            sp.dma_start(c_sb[:, :], a["c"]).then_inc(s_c, 16)
            load_x(0)
            sp.dma_start(ident[:, :], a["ident"]).then_inc(s_ident, 16)
            load_wmod(0)
            for tc in range(1, NCH):
                load_x(tc)
            load_attn(0)
            load_wmod(1)
            for dst, name in ((identb, "identb"), (neg_m, "neg_m"), (neg_e, "neg_e"),
                              (gate_s, "gate_s"), (up_s, "up_s")):
                sp.dma_start(dst[:, :], a[name]).then_inc(s_const, 16)
            sp.dma_start(down_s[:, :], a["down_s"].partition_broadcast(P)).then_inc(s_const, 16)
            sp.dma_start(gate_w[:, :, :], a["gate_w"].rearrange("(k p) n -> p k n", p=P)).then_inc(s_const, 16)
            sp.dma_start(tri[:, :, :], a["tri"].partition_broadcast(P)).then_inc(s_const, 16)
            sp.dma_start(esel[:, :, :], a["esel"]).then_inc(s_const, 16)
            load_ffn(0)
            for y in range(NLAY):
                for tc in range(NCH):
                    for side in range(2):
                        for f in range(KD):
                            k = (y * NCH + tc) * 4 + side * KD + f
                            sp.wait_ge(s_l, k + 1)
                            sp.dma_start(parts[side, :, f * P:(f + 1) * P, tc * CH:(tc + 1) * CH].rearrange("k f t -> f k t"),
                                         st_p[k % 3]).then_inc(s_split[k % 3], 16)
                    if y == 1 or tc == NCH - 1:
                        for b in range(3):
                            jobs = len([k for k in range(4 * (y * NCH + tc + 1)) if k % 3 == b])
                            sp.wait_ge(s_split[b], 16 * jobs)
                    if y == 1:
                        if tc == 0:
                            load_rows(y, 0)
                        load_key_chunk(tc)
                sp.wait_ge(s_mod, NLAY)
                for g in range(y, NG):
                    load_rows(y, g)
                    load_keys(g)
                    if g == NG - 2:
                        place_maximum(y, 0)
                if y == 1:
                    sp.wait_ge(s_u, K0[1])
                    load_ffn(1)
                for s, n, k, _blocks in slot_walk(y):
                    if k == 0 and n > 0:
                        if n + 3 < NU:
                            load_rows(y, n + 3)
                    if s >= 0 and mt_slot(y, n, k) is not None:
                        place_maximum(y, mt_slot(y, n, k))
                sp.wait_ge(s_pv, S0[y + 1])
                load_down(y)
                if y == 0:
                    sp.wait_ge(s_op, 8)
                    load_attn(1)
            for t in range(NT):
                sp.wait_ge(s_xd, NT + t + 1)
                sp.dma_start(a["out"][t * P:(t + 1) * P, :], x_sb[:, t, :]).then_inc(s_out, 16)
            sp.wait_ge(s_out, 16 * NT)

        @block.gpsimd
        def _(pool):
            chain = [0]

            def link(ins):
                chain[0] += 1
                ins.then_inc(s_pool, 1)
                pool.wait_ge(s_pool, chain[0])

            def ln(q):
                for tc in range(NCH):
                    j = q * NCH + tc
                    pool.wait_ge(s_mv, j + 1)
                    if j:
                        pool.wait_ge(s_rstd, j)
                    link(nc.gpsimd.tensor_scalar(vare[:, :], mv[:, tc % 2, :, 1], EPS, None, ALU.add))
                    if j >= 2:
                        pool.wait_ge(s_xh, j - 1)
                    nc.gpsimd.tensor_tensor(rstd[:, tc % 2, :], vare[:, :], half[:, :], ALU.pow).then_inc(s_rstd, 1)

            def scale_wo(y):
                pool.wait_ge(s_mod, y + 1)
                pool.wait_ge(s_wattn, 128 * (y + 1))
                for g in range(KD):
                    link(nc.gpsimd.tensor_tensor(w_o[:, g, :], w_o[:, g, :], gab[:, y, 0:D], ALU.mult))
                nc.gpsimd.tensor_tensor(b_o[:, :], b_o[:, :], gab[:, y, 0:D], ALU.mult).then_inc(s_wo, 1)
                pool.wait_ge(s_wo, y + 1)

            def add_bias(y):
                pool.wait_ge(s_xh, (2 * y + 1) * NCH)
                for t in range(NT):
                    ins = nc.gpsimd.tensor_tensor(x_sb[:, t, :], x_sb[:, t, :], b_o[:, :], ALU.add)
                ins.then_inc(s_obg, 1)

            def scale_down(y):
                pool.wait_ge(s_wdown, 32 * (y + 1))
                if y == 0:
                    pool.wait_ge(s_const, 144)
                    link(nc.gpsimd.tensor_tensor(gab[:, y, D:2 * D], gab[:, y, D:2 * D], down_s[:, :], ALU.mult))
                for c in range(NC[y]):
                    f = fsize(y, c)
                    ins = nc.gpsimd.tensor_tensor(down[0:f, c, :], down[0:f, c, :], gab[0:f, y, D:2 * D], ALU.mult)
                ins.then_inc(s_wd, 1)

            link(nc.gpsimd.memset(half[:, :], -0.5))
            for y in range(NLAY):
                ln(2 * y)
                scale_wo(y)
                add_bias(y)
                ln(2 * y + 1)
                scale_down(y)

        @block.tensor
        def _(pe):
            def modulation(y):
                pe.wait_ge(s_cs, 1)
                pe.wait_ge(s_wmod[y], 16)
                for i, col in enumerate((2, 5)):
                    for k in range(KD):
                        mm = pe.matmul(bank(2 + 2 * y)[:, i * D:(i + 1) * D], csb[:, y * KD + k, :],
                                       wmod[y][:, k, col * D:(col + 1) * D], start=(k == 0), stop=(k == KD - 1))
                for i in range(8):
                    col = (0, 1, 3, 4)[i // 2] * D + (i % 2) * P
                    for k in range(KD):
                        mm = pe.matmul(bank(3 + 2 * y)[:, i:i + 1], wmod[y][:, k, col:col + P],
                                       cs[:, y * KD + k:y * KD + k + 1], start=(k == 0), stop=(k == KD - 1))
                mm.then_inc(s_modp, 1)

            mb = [0]

            def max_block(y, n, h, r, q):
                i, g = n // NG, n % NG
                b = mb[0]
                mb[0] += 1
                if n == 0 and (h, r) == (0, 0) and (y or q == 0):
                    if q == 0:
                        pe.wait_ge(s_row[g], 112 * (y * NCH + 1))
                    if y:
                        pe.wait_ge(s_chunk[q], 112)
                    else:
                        pe.wait_ge(s_key[g], 112)
                elif n and (h, r, q) == (0, 0, 0):
                    pe.wait_ge(s_row[g], 112 * (y * NCH + i + 1))
                    if g:
                        pe.wait_ge(s_key[g], 112 * (y + 1))
                if EARLY0 <= b < EARLY1:
                    pe.wait_ge(s_mr, b - 1)
                elif b >= 3:
                    pe.wait_ge(s_mr, EARLY1 if EARLY1 <= b < EARLY1 + 2 else b - 2)
                last = CAUSAL[y] and q == i
                w = (r + 1) * P if last else CH
                out = bank(mb_bank(b))
                mm = pe.matmul(out[:, 0:w], rows[0:KS, g, h, r * P:(r + 1) * P],
                               keys[0:KS, g * HG + h, q * CH:q * CH + w], start=True, stop=not last)
                if last:
                    mm = pe.matmul(out[:, w - P:w], identb[:, :], neg_m[:, :], start=False, stop=True)
                mm.then_inc(s_mb, 1)

            def early_blocks(count, tc):
                if count:
                    pe.wait_ge(s_qf, 4 * (NCH + tc))
                for _ in range(count):
                    max_block(1, *plans[1][0][mb[0] - M0[1]])

            def ln(q, tc, c):
                j = q * NCH + tc
                y = q // 2
                pe.wait_ge(s_xh, j + 1)
                if q == 0:
                    if tc:
                        pe.wait_ge(s_hte, 2 * (j - 1) + c + 1)
                elif q == 2:
                    pe.wait_ge(s_mr, mb[0])
                    if tc:
                        pe.wait_ge(s_qf, 4 * (NCH + tc))
                elif tc < NCH - 1:
                    if c == 0:
                        pe.wait_ge(s_on, y * NU + NG * (tc + 1) + 1)
                    else:
                        pe.wait_ge(s_hte, 2 * j + 1)
                else:
                    pe.wait_ge(s_on, (y + 1) * NU)
                    pe.wait_ge(s_xa, 8 * (y + 1))
                for t in range(TPC):
                    mm = pe.transpose(bank(ln_bank(q, tc, c))[:, t * P:(t + 1) * P],
                                      xh[:, xh_buf(q, tc), t, c * P:(c + 1) * P], ident[:, :])
                mm.then_inc(s_tr, 1)

            def proj(y, tc):
                if tc == 0:
                    pe.wait_ge(s_wattn, 128 * (y + 1))
                    pe.wait_ge(s_modc, 1)
                if y:
                    pe.wait_ge(s_mr, mb[0])
                pe.wait_ge(s_hte, 16 * y + 2 * (tc + 1))
                tok = slice(tc * CH, (tc + 1) * CH)
                for side, w in enumerate((w_row, w_col)):
                    for f in range(KD):
                        j = (y * NCH + tc) * 4 + side * KD + f
                        if j >= 2:
                            pe.wait_ge(s_qf, j - 1)
                        for k in range(KD):
                            mm = pe.matmul(bank(2 + 2 * y + j % 2), w[:, k, f * P:(f + 1) * P], hT[:, k, tok],
                                           start=(k == 0), stop=(k == KD - 1))
                        mm.then_inc(s_pj, 1)

            def value(y, t):
                v = y * NT + t
                if t == 0:
                    pe.wait_ge(s_qf, 16 * (y + 1))
                if v >= 2:
                    pe.wait_ge(s_ve, v - 1)
                for k in range(KD):
                    mm = pe.matmul(bank(6 + v % 2)[:, 0:D], hT[:, k, t * P:(t + 1) * P], w_v[:, k, :],
                                   start=(k == 0), stop=(k == KD - 1))
                mm.then_inc(s_vp, 1)

            def sums_transpose(y, n):
                pe.wait_ge(s_oc, y * NU + n + 1)
                for t in range(TPC):
                    mm = pe.transpose(bank(6 + n % 2)[:, t * P:(t + 1) * P], out_sb[:, t * P:(t + 1) * P], ident[:, :])
                mm.then_inc(s_ft, 1)

            def back_transpose(y, i, half_):
                pe.wait_ge(s_on, y * NU + NG * (i + 1))
                if half_:
                    pe.wait_ge(s_ac, 2 * (y * NCH + i) + 1)
                for f in range(KD):
                    for r in range(2):
                        mm = pe.transpose(bank(7)[:, (2 * f + r) * P:(2 * f + r + 1) * P],
                                          attn_n[:, 2 * half_ + r, f * P:(f + 1) * P], ident[:, :])
                mm.then_inc(s_bt, 1)

            def output(y, i, half_):
                if half_ == 0:
                    pe.wait_ge(s_ac, 2 * (y * NCH + i) + 2)
                    pe.wait_ge(s_wo, y + 1)
                else:
                    pe.wait_ge(s_xa, 8 * y + 2 * i + 1)
                for r in range(2):
                    t = 2 * half_ + r
                    for f in range(KD):
                        mm = pe.matmul(bank(7)[:, r * D:(r + 1) * D], attn_t[:, f, t * P:(t + 1) * P], w_o[:, f, :],
                                       start=(f == 0), stop=(f == KD - 1))
                mm.then_inc(s_op, 1)

            def attention(y):
                def max_transpose(n):
                    u = y * NU + n
                    pe.wait_ge(s_mp, u + 1)
                    if n < 2:
                        pe.wait_ge(s_ve, NT * (y + 1))
                    elif n % NG == 1:
                        pe.wait_ge(s_xa, 8 * y + 2 * (n // NG))
                    elif n % NG == 2 and n > 2:
                        pe.wait_ge(s_hte, 16 * y + 8 + 2 * (n // NG))
                    elif n >= 2:
                        pe.wait_ge(s_on, u - 1)
                    for h in range(HG):
                        for r in range(TPC):
                            mm = pe.matmul(psum[32 * h:32 * h + 32, 6 + n % 2, r * P:(r + 1) * P],
                                           mp[:, h * TPC + r, :], identb[:, :], start=True, stop=True)
                    mm.then_inc(s_mt, 1)

                def scores(s, n, jt, h):
                    i, g = n // NG, n % NG
                    e = HG * (S0[y] + s) + h
                    if jt == 0 and h == 0:
                        pe.wait_ge(s_mrow, 64 * (y * NU + n + 1))
                    if n == NU - 1 and jt == 0 and h == 0:
                        pe.wait_ge(s_mr, M0[y + 1])
                    if n == NU - 1 and HG * jt + h >= 6:
                        pe.wait_ge(s_p, e - 5)
                    elif e >= 3:
                        pe.wait_ge(s_p, e - 2)
                    off = max(0, jt - TPC * i) * P if CAUSAL[y] else 0
                    diag = CAUSAL[y] and jt >= TPC * i
                    out = bank(score_bank(n, e))
                    mm = pe.matmul(out[:, off:CH], keys[0:KS, g * HG + h, jt * P:(jt + 1) * P],
                                   rows[0:KS, g, h, off:CH], start=True, stop=not diag)
                    if diag:
                        mm = pe.matmul(out[:, off:off + P], identb[:, :], neg_e[:, :], start=False, stop=True)
                    mm.then_inc(s_e, 1)

                def values(s, n, jt):
                    i, g = n // NG, n % NG
                    pe.wait_ge(s_p, HG * (S0[y] + s + 1))
                    if jt == 0:
                        pe.wait_ge(s_mtc, y * NU + n + 1)
                    off = max(0, jt - TPC * i) * P if CAUSAL[y] else 0
                    for h in range(HG):
                        mm = pe.matmul(psum[32 * h:32 * h + VW, 6 + n % 2, off:CH], v_sb[:, jt, g * HG + h, :],
                                       probs[:, (S0[y] + s) % 2, h, off:CH], start=(jt == 0), stop=(jt == steps_of(y, n) - 1))
                    mm.then_inc(s_pv, 1)

                pe.wait_ge(s_qf, 16 * (y + 1))
                if y == 0:
                    pe.wait_ge(s_hte, 2 * NCH)
                for what, w in prologue(y):
                    if what == "value":
                        value(y, w)
                    else:
                        max_block(y, *w)
                before = None
                for s, n, k, blocks in slot_walk(y):
                    if s == -1:
                        max_transpose(0)
                    quarter = [len(blocks) * m // 4 for m in range(5)]
                    for m in range(4):
                        for b in blocks[quarter[m]:quarter[m + 1]]:
                            max_block(y, *b)
                        if s >= 0 and m in ((0,) if n == NU - 1 else (0, 2)):
                            for h in range(m, HG if n == NU - 1 else m + 2):
                                scores(s, n, k, h)
                        if m == 1 and before:
                            values(*before)
                    before = (s, n, k) if s >= 0 else None
                    if s >= 0:
                        if k == 1 and n > 0:
                            sums_transpose(y, n - 1)
                        if back_slot(n, k):
                            back_transpose(y, *back_slot(n, k))
                        if oproj_slot(n, k):
                            output(y, *oproj_slot(n, k))
                        if ln_slot(n, k):
                            ln(2 * y + 1, *ln_slot(n, k))
                        if mt_slot(y, n, k) is not None:
                            max_transpose(mt_slot(y, n, k))
                values(*before)

            def logits(part):
                lo, hi = ROUTE[part]
                pe.wait_ge(s_hte, 24 + 2 * (hi // TPC))
                for t in range(lo, hi):
                    for k in range(KD):
                        mm = pe.matmul(bank(LB[part])[:, t * NE:(t + 1) * NE], hT[:, k, t * P:(t + 1) * P], gate_w[:, k, :],
                                       start=(k == 0), stop=(k == KD - 1))
                mm.then_inc(s_lg, 1)

            def weights(part):
                pe.wait_ge(s_rp, part + 1)
                for tc in range(ROUTE[part][0] // TPC, ROUTE[part][1] // TPC):
                    if tc:
                        pe.wait_ge(s_wt, tc)
                    for r in range(TPC):
                        t = tc * TPC + r
                        mm = pe.matmul(psum[0:3 * NE, WB[part], r * P:(r + 1) * P],
                                       r_p[:, t, :, :].rearrange("p k e -> p (k e)"), identb[:, :], start=True, stop=True)
                    mm.then_inc(s_rt, 1)

            def ffn(y):
                pe.wait_ge(s_wffn, 32 * (y + 1))
                pe.wait_ge(s_mr, M0[y + 1])
                for what, tc, c, k in ffn_walk(y):
                    tok = slice(tc * CH, (tc + 1) * CH)
                    if what == "hid":
                        f = fsize(y, c)
                        pe.wait_ge(s_hte, 16 * y + 8 + 2 * (tc + 1))
                        if k - K0[y] >= 2:
                            pe.wait_ge(s_sil, k - 1)
                        for d in range(KD):
                            mm = pe.matmul(psum[0:f, k % 2, :], up_gate[y][0][:, d, c * P:c * P + f], hT[:, d, tok],
                                           start=(d == 0), stop=(d == KD - 1))
                        mm.then_inc(s_g, 1)
                        early = EARLY.get((tc, c), (0, 0)) if y == 0 else (0, 0)
                        proj_done = tc - 1 if c < 4 else tc
                        early_blocks(early[0], proj_done)
                        if k - K0[y] >= 2:
                            pe.wait_ge(s_hid, k - 1)
                        for d in range(KD):
                            mm = pe.matmul(psum[0:f, 2 + k % 2, :], up_gate[y][1][:, d, c * P:c * P + f], hT[:, d, tok],
                                           start=(d == 0), stop=(d == KD - 1))
                        if y == 1 and c < RC:
                            if tc == 0:
                                pe.wait_ge(s_le, 1)
                            pe.wait_ge(s_wt, NCH if tc == NCH - 1 else NCH - 1)
                            mm = pe.matmul(bank(4 + k % 2), esel[:, c, :], wT[0:3 * NE, tok], start=True, stop=True)
                        mm.then_inc(s_u, 1)
                        early_blocks(early[1], proj_done)
                    elif what == "down":
                        pe.wait_ge(s_hid, k)
                        pe.wait_ge(s_wd, y + 1)
                        for r in range(TPC):
                            j = y * NT + tc * TPC + r
                            if tc == 0 and r < 2:
                                pe.wait_ge(s_hte, 16 * (y + 1))
                                if y == 1:
                                    pe.wait_ge(s_le, 2)
                                    pe.wait_ge(s_wt, NCH)
                            else:
                                pe.wait_ge(s_xd, j - 1)
                            for cc in range(NC[y]):
                                f = fsize(y, cc)
                                mm = pe.matmul(bank(6 + j % 2)[:, 0:D], hid[y][tc % 2][0:f, cc, r * P:(r + 1) * P],
                                               down[0:f, cc, :], start=(cc == 0), stop=(cc == NC[y] - 1))
                            mm.then_inc(s_dn, 1)
                            if y == 0 and tc == NCH - 1:
                                early_blocks(EARLY_DOWN, tc)
                    elif what == "ln":
                        q = ln_of(y, tc, k)
                        for cc in range(KD):
                            ln(q, tc, cc)
                    elif what == "proj":
                        proj(1, tc)
                    elif what == "logits":
                        logits(tc)
                    elif what == "weights":
                        weights(tc)
                    elif c == 0:
                        sums_transpose(y, NU - 1)
                    elif c < 3:
                        back_transpose(y, NCH - 1, c - 1)
                    else:
                        output(y, NCH - 1, c - 3)

            for y in range(NLAY):
                if y == 0:
                    pe.wait_ge(s_ident, 16)
                    for tc in range(NCH):
                        for c in range(KD):
                            ln(0, tc, c)
                        if tc == 0:
                            modulation(0)
                        else:
                            proj(0, tc - 1)
                        if tc == 2:
                            modulation(1)
                    proj(0, NCH - 1)
                    pe.wait_ge(s_const, 144)
                    pe.wait_ge(s_modc, NLAY)
                else:
                    pe.wait_ge(s_sil, K0[1])
                    pe.wait_ge(s_hid, K0[1])
                    pe.wait_ge(s_xd, NT)
                attention(y)
                pe.wait_ge(s_p, HG * S0[y + 1])
                ffn(y)

        @block.scalar
        def _(act):
            chain = [0]

            def link(ins):
                chain[0] += 1
                ins.then_inc(s_act, 1)
                act.wait_ge(s_act, chain[0])

            act.wait_ge(s_c, 16)
            nc.scalar.activation(ce[:, :], c_sb[:, :], ACT.Exp, scale=-1.0).then_inc(s_ce, 1)
            act.wait_ge(s_modc, 1)

            def ln(q, tc, c):
                y = q // 2
                if tc == 0 and c == 0 and q % 2:
                    act.wait_ge(s_vp, NT * (y + 1))
                if tc == 0 and c == 0 and q == 2:
                    act.wait_ge(s_modc, NLAY)
                if c == 0 and q == 2:
                    act.wait_ge(s_u, hid_end(0, tc))
                act.wait_ge(s_tr, 2 * (q * NCH + tc) + c + 1)
                i = 4 * (q % 2) + c
                nc.scalar.activation(hT[:, c, tc * CH:(tc + 1) * CH], bank(ln_bank(q, tc, c)), ACT.Identity,
                                     bias=modc[:, y, i:i + 1], scale=modc[:, y, i + 2:i + 3]).then_inc(s_hte, 1)

            def proj(y, tc):
                act.wait_ge(s_bs, y + 1)
                for side in range(2):
                    for f in range(KD):
                        k = (y * NCH + tc) * 4 + side * KD + f
                        b = k % 3
                        act.wait_ge(s_pj, k + 1)
                        if k >= 3:
                            act.wait_ge(s_l, k - 2)
                            act.wait_ge(s_split[b], 16 * (k // 3))
                        nc.scalar.activation(st_f[b], bank(2 + 2 * y + k % 2), ACT.Identity,
                                             bias=(b_row, b_col)[side][:, f:f + 1],
                                             scale=(1.0, SCALES[y])[side]).then_inc(s_qf, 1)
                        act.wait_ge(s_qf, k + 1)
                        nc.scalar.activation(st_p[b][:, 0, :], st_f[b], ACT.Identity).then_inc(s_h, 1)

            def attention(y):
                for s, n, k, _blocks in slot_walk(y):
                    if s >= 0:
                        i = n // NG
                        off = max(0, k - TPC * i) * P if CAUSAL[y] else 0
                        for h in range(HG):
                            e = HG * (S0[y] + s) + h
                            act.wait_ge(s_e, e + 1)
                            if S0[y] + s >= 2:
                                act.wait_ge(s_pv, S0[y] + s - 1)
                            nc.scalar.activation(probs[:, (S0[y] + s) % 2, h, off:CH], psum[:, score_bank(n, e), off:CH],
                                                 ACT.Exp).then_inc(s_p, 1)
                            if h == 1:
                                if k and back_slot(n, k - 1):
                                    copy_features(y, *back_slot(n, k - 1))
                                if k and ln_slot(n, k - 1):
                                    ln(2 * y + 1, *ln_slot(n, k - 1))
                                if k and mt_slot(y, n, k - 1) is not None:
                                    copy_maximum(y, mt_slot(y, n, k - 1))
                        if k == 0 and n > 0:
                            copy_out(y, n - 1)
                    else:
                        copy_maximum(y, 0)
                copy_out(y, NU - 1)

            def copy_maximum(y, m):
                act.wait_ge(s_mt, y * NU + m + 1)
                if y * NU + m:
                    act.wait_ge(s_mrow, 64 * (y * NU + m))
                nc.scalar.activation(mrow_t[:, :], bank(6 + m % 2), ACT.Identity).then_inc(s_mtc, 1)

            def copy_features(y, i, half_):
                act.wait_ge(s_bt, 2 * (y * NCH + i) + half_ + 1)
                if y * NCH + i and not half_:
                    act.wait_ge(s_op, 2 * (y * NCH + i))
                if i and not half_:
                    act.wait_ge(s_tr, 16 * y + 8 + 2 * i)
                nc.scalar.activation(attn_t[:, :, half_ * 2 * P:(half_ + 1) * 2 * P],
                                     bank(7).rearrange("p (k t) -> p k t", k=KD), ACT.Identity).then_inc(s_ac, 1)

            def copy_out(y, n):
                u = y * NU + n
                act.wait_ge(s_pv, unit_steps(y, n))
                if u:
                    act.wait_ge(s_ft, u)
                nc.scalar.activation(out_sb[:, :], bank(6 + n % 2), ACT.Identity).then_inc(s_oc, 1)

            def ffn(y):
                for what, tc, c, k in ffn_walk(y):
                    if what == "hid":
                        f = fsize(y, c)
                        act.wait_ge(s_g, k + 1)
                        if k >= 2:
                            act.wait_ge(s_hid, k - 1)
                        nc.scalar.activation(sil[k % 2][0:f, :], psum[0:f, k % 2, :], ACT.Silu,
                                             scale=gate_s[0:f, c:c + 1] if y == 0 else 1.0).then_inc(s_sil, 1)
                    elif what == "ln":
                        for cc in range(KD):
                            ln(ln_of(y, tc, k), tc, cc)
                    elif what == "proj":
                        proj(1, tc)
                    elif what == "logits":
                        lo, hi = ROUTE[tc]
                        act.wait_ge(s_lg, tc + 1)
                        nc.scalar.activation(r_s[:, lo:hi, :], bank(LB[tc])[:, lo * NE:hi * NE].rearrange("p (t e) -> p t e", e=NE),
                                             ACT.Exp, scale=-1.0).then_inc(s_le, 1)
                    elif what == "tail" and c in (1, 2):
                        copy_features(y, NCH - 1, c - 1)

            for y in range(NLAY):
                if y == 0:
                    for tc in range(NCH):
                        for c in range(KD):
                            ln(0, tc, c)
                        if tc:
                            proj(0, tc - 1)
                    proj(0, NCH - 1)
                attention(y)
                ffn(y)

        @block.vector
        def _(dve):
            chain = [0]

            def link(ins):
                chain[0] += 1
                ins.then_inc(s_dve, 1)
                dve.wait_ge(s_dve, chain[0])

            V = nc.vector
            link(V.memset(mp[:, :, :], 0.0))
            dve.wait_ge(s_ce, 1)
            link(V.tensor_scalar(ce[:, :], ce[:, :], 1.0, None, ALU.add))
            link(V.reciprocal(ce[:, :], ce[:, :]))
            link(V.tensor_tensor(cs[:, :], ce[:, :], c_sb[:, :], ALU.mult))
            for k in range(2 * KD):
                ins = V.tensor_copy(csb[:, k, :], cs[:, k:k + 1].to_broadcast([P, P]))
            ins.then_inc(s_cs, 1)
            def shifts(y):
                dve.wait_ge(s_modp, y + 1)
                g = gab[:, y, :]
                link(V.tensor_copy(g, bank(2 + 2 * y)))
                link(V.tensor_copy(modc[:, y, :], bank(3 + 2 * y)[:, 0:8]))
                for i in (2, 6):
                    ins = V.tensor_scalar(modc[:, y, i:i + 2], modc[:, y, i:i + 2], 1.0, None, ALU.add)
                ins.then_inc(s_modc, 1)

            def gates(y):
                g = gab[:, y, :]
                link(V.tensor_scalar(gtmp[:, 0, :], g, 0.0, 2.0, ALU.is_ge, ALU.mult))
                link(V.scalar_tensor_tensor(gtmp[:, 1, :], g, -1.0, g, ALU.mult, ALU.max))
                link(V.tensor_scalar(gtmp[:, 1, :], gtmp[:, 1, :], 0.25, None, ALU.max))
                V.scalar_tensor_tensor(g, gtmp[:, 0, :], -1.0, gtmp[:, 1, :], ALU.add, ALU.mult).then_inc(s_mod, 1)

            def stats_of(q, tc):
                if q == 0:
                    dve.wait_ge(s_x[tc], 16)
                elif q % 2 == 1:
                    dve.wait_ge(s_xa, 8 * (q // 2) + 2 * (tc + 1))
                else:
                    dve.wait_ge(s_xd, TPC * (tc + 1))
                j = q * NCH + tc
                for t in range(TPC):
                    ins = V.bn_stats(stats[:, t, :], x_sb[:, tc * TPC + t, :])
                link(ins)
                if j >= 2:
                    dve.wait_ge(s_xh, j - 1)
                    dve.wait_ge(s_rstd, j - 1)
                for t in range(TPC):
                    ins = V.bn_aggr(mv[:, tc % 2, t, :], stats[:, t, :])
                ins.then_inc(s_mv, 1)
                dve.wait_ge(s_mv, j + 1)

            def normed(q, tc):
                j = q * NCH + tc
                dve.wait_ge(s_rstd, j + 1)
                if j >= 2:
                    dve.wait_ge(s_tr, 2 * (j if q % 2 else j - 1))
                for t in range(TPC):
                    ins = V.tensor_scalar(xh[:, xh_buf(q, tc), t, :], x_sb[:, tc * TPC + t, :], mv[:, tc % 2, t, 0:1],
                                          rstd[:, tc % 2, t:t + 1], ALU.subtract, ALU.mult)
                ins.then_inc(s_xh, 1)

            def scale_bias(y):
                dve.wait_ge(s_wattn, 128 * (y + 1))
                if y:
                    dve.wait_ge(s_qf, 16)
                V.tensor_scalar(b_col[:, :], b_colr[:, :], SCALES[y], None, ALU.mult).then_inc(s_bs, 1)

            def split(y, tc):
                for k in range(4 * (y * NCH + tc), 4 * (y * NCH + tc) + 4):
                    b = k % 3
                    dve.wait_ge(s_h, k + 1)
                    link(V.tensor_tensor(st_r[b], st_f[b], st_p[b][:, 0, :], ALU.subtract))
                    link(V.tensor_copy(st_p[b][:, 1, :], st_r[b]))
                    V.tensor_tensor(st_p[b][:, 2, :], st_r[b], st_p[b][:, 1, :], ALU.subtract).then_inc(s_l, 1)

            def ones(y):
                if y == 1:
                    dve.wait_ge(s_dn, NT)
                link(V.memset(v_sb[:, :, :, HD], 1.0))

            def value(y, t):
                v = y * NT + t
                dve.wait_ge(s_vp, v + 1)
                V.tensor_tensor(v_sb[:, t, :, 0:HD], bank(6 + v % 2)[:, 0:D].rearrange("p (h c) -> p h c", h=H),
                                b_v[:, :].rearrange("p (h c) -> p h c", h=H), ALU.add).then_inc(s_ve, 1)

            def normalise(y, n):
                u, g = y * NU + n, n % NG
                if g == 0 and n > 0:
                    dve.wait_ge(s_bt, 2 * (y * NCH + n // NG))
                dve.wait_ge(s_ft, u + 1)
                if u:
                    dve.wait_ge(s_on, u)
                sums = bank(6 + n % 2).rearrange("p (t h c) -> p t h c", t=TPC, h=HG)
                link(V.reciprocal(rden[:, :, :], sums[:, :, :, HD]))
                V.tensor_tensor(attn_n[:, :, g * GF:(g + 1) * GF].rearrange("p t (h c) -> p t h c", h=HG),
                                sums[:, :, :, 0:HD], rden[:, :, :].unsqueeze(3).to_broadcast([P, TPC, HG, HD]),
                                ALU.mult).then_inc(s_on, 1)

            def add_output(y, i, half_):
                j = 8 * y + 2 * i + half_
                dve.wait_ge(s_obg, y + 1)
                dve.wait_ge(s_op, j + 1)
                t = TPC * i + 2 * half_
                V.tensor_tensor(x_sb[:, t:t + 2, :], bank(7).rearrange("p (t d) -> p t d", t=2), x_sb[:, t:t + 2, :],
                                ALU.add).then_inc(s_xa, 1)

            mb = [0]

            def reduce_block(y, n, h, r, q):
                b = mb[0]
                mb[0] += 1
                chunks = n // NG + 1 if CAUSAL[y] else NCH
                last = CAUSAL[y] and q == n // NG
                w = (r + 1) * P if last else CH
                dve.wait_ge(s_mb, b + 1)
                V.tensor_reduce(mpart[:, h * TPC + r, q:q + 1], bank(mb_bank(b))[:, 0:w], AX.X, ALU.max).then_inc(s_mr, 1)
                if (h, r, q) == (HG - 1, TPC - 1, chunks - 1):
                    dve.wait_ge(s_mr, b + 1)
                    u = y * NU + n
                    link(V.tensor_reduce(mx[:, :], mpart[:, :, 0:chunks], AX.X, ALU.max))
                    link(V.tensor_scalar(mx[:, :], mx[:, :], ROUND, -ROUND, ALU.add, ALU.add))
                    if u:
                        dve.wait_ge(s_mt, u)
                    link(V.tensor_scalar(mp[:, :, 0], mx[:, :], -1.0, None, ALU.mult))
                    V.scalar_tensor_tensor(mp[:, :, 1], mx[:, :], -1.0, mp[:, :, 0], ALU.mult, ALU.subtract).then_inc(s_mp, 1)

            def attention(y):
                for what, w in prologue(y):
                    if what == "value":
                        value(y, w)
                    else:
                        reduce_block(y, *w)
                for s, n, k, blocks in slot_walk(y):
                    if s >= 0 and k == 2 and n > 0:
                        normalise(y, n - 1)
                    if s >= 0 and k and oproj_slot(n, k - 1):
                        add_output(y, *oproj_slot(n, k - 1))
                        if oproj_slot(n, k - 1)[1]:
                            stats_of(2 * y + 1, n // NG - 1)
                    for b in blocks:
                        reduce_block(y, *b)
                    if s >= 0 and n % NG == 0 and n > 0 and k == 7:
                        normed(2 * y + 1, n // NG - 1)

            def router(part):
                dve.wait_ge(s_le, part + 1)
                lo, hi = ROUTE[part]
                n = hi - lo
                ts = slice(lo, hi)
                link(V.tensor_scalar(r_s[:, ts, :], r_s[:, ts, :], 1.0, None, ALU.add))
                link(V.reciprocal(r_s[:, ts, :], r_s[:, ts, :]))
                mine = r_s[:, ts, :].unsqueeze(3).to_broadcast([P, n, NE, NE])
                other = r_s[:, ts, :].unsqueeze(2).to_broadcast([P, n, NE, NE])
                low = tri[:, :, :].unsqueeze(1).to_broadcast([P, n, NE, NE])
                link(V.tensor_tensor(r_gt[:, ts, :, :], other, mine, ALU.is_gt))
                link(V.tensor_tensor(r_eq[:, ts, :, :], other, mine, ALU.is_equal))
                link(V.tensor_tensor(r_eq[:, ts, :, :], r_eq[:, ts, :, :], low, ALU.mult))
                link(V.tensor_tensor(r_gt[:, ts, :, :], r_gt[:, ts, :, :], r_eq[:, ts, :, :], ALU.add))
                link(V.tensor_reduce(r_rank[:, ts, :], r_gt[:, ts, :, :], AX.X, ALU.add))
                link(V.tensor_scalar(r_rank[:, ts, :], r_rank[:, ts, :], 2.0, None, ALU.is_lt))
                link(V.tensor_tensor(r_w[:, ts, :], r_rank[:, ts, :], r_s[:, ts, :], ALU.mult))
                link(V.tensor_reduce(r_sum[:, ts], r_w[:, ts, :], AX.X, ALU.add))
                link(V.tensor_scalar(r_sum[:, ts], r_sum[:, ts], 1e-20, None, ALU.add))
                link(V.reciprocal(r_inv[:, ts], r_sum[:, ts]))
                link(V.tensor_scalar(r_inv[:, ts], r_inv[:, ts], 2.5, None, ALU.mult))
                link(V.tensor_tensor(r_w[:, ts, :], r_w[:, ts, :], r_inv[:, ts].unsqueeze(2).to_broadcast([P, n, NE]), ALU.mult))
                link(V.tensor_copy(r_p[:, ts, 0, :], r_w[:, ts, :]))
                link(V.tensor_tensor(r_lo[:, ts, :], r_w[:, ts, :], r_p[:, ts, 0, :], ALU.subtract))
                link(V.tensor_copy(r_p[:, ts, 1, :], r_lo[:, ts, :]))
                V.tensor_tensor(r_p[:, ts, 2, :], r_lo[:, ts, :], r_p[:, ts, 1, :], ALU.subtract).then_inc(s_rp, 1)

            def weights(part):
                for tc in range(ROUTE[part][0] // TPC, ROUTE[part][1] // TPC):
                    dve.wait_ge(s_rt, tc + 1)
                    V.tensor_copy(wT[0:3 * NE, tc * CH:(tc + 1) * CH], psum[0:3 * NE, WB[part], :]).then_inc(s_wt, 1)

            def ffn(y):
                def early_blocks(count):
                    for _ in range(count):
                        reduce_block(1, *plans[1][0][mb[0] - M0[1]])

                first_hid = {}
                for what, tc, c, k in ffn_walk(y):
                    if what == "hid":
                        f = fsize(y, c)
                        early = EARLY.get((tc, c), (0, 0)) if y == 0 else (0, 0)
                        early_blocks(early[0])
                        dve.wait_ge(s_sil, k + 1)
                        dve.wait_ge(s_u, k + 1)
                        if first_hid.setdefault(tc, k) == k and tc >= 2:
                            dve.wait_ge(s_dn, y * NT + (tc - 1) * TPC)
                        dst, up = hid[y][tc % 2][0:f, c, :], psum[0:f, 2 + k % 2, :]
                        if y == 0:
                            V.scalar_tensor_tensor(dst, up, up_s[0:f, c:c + 1], sil[k % 2][0:f, :], ALU.mult, ALU.mult).then_inc(s_hid, 1)
                        elif c < RC:
                            link(V.tensor_tensor(utmp[k % 2], up, sil[k % 2], ALU.mult))
                            V.tensor_tensor(dst, bank(4 + k % 2), utmp[k % 2], ALU.mult).then_inc(s_hid, 1)
                        else:
                            V.tensor_tensor(dst, up, sil[k % 2][0:f, :], ALU.mult).then_inc(s_hid, 1)
                        early_blocks(early[1])
                    elif what == "down":
                        for r in range(TPC):
                            j = y * NT + tc * TPC + r
                            dve.wait_ge(s_dn, j + 1)
                            t = tc * TPC + r
                            V.tensor_tensor(x_sb[:, t, :], bank(6 + j % 2)[:, 0:D], x_sb[:, t, :], ALU.add).then_inc(s_xd, 1)
                            if y == 0 and tc == NCH - 1:
                                early_blocks(EARLY_DOWN)
                        if y == 0:
                            stats_of(2, tc)
                            normed(2, tc)
                    elif what == "proj":
                        split(1, tc)
                    elif what == "logits":
                        router(tc)
                    elif what == "weights":
                        weights(tc)
                    elif what == "ln" and y == 0 and ln_of(y, tc, k) == 1:
                        scale_bias(1)
                    elif what == "tail" and c == 0:
                        normalise(y, NU - 1)
                    elif what == "tail" and c == 3:
                        add_output(y, NCH - 1, 0)
                    elif what == "tail" and c == 4:
                        add_output(y, NCH - 1, 1)
                        stats_of(2 * y + 1, NCH - 1)
                        normed(2 * y + 1, NCH - 1)

            stats_of(0, 0)
            normed(0, 0)
            shifts(0)
            stats_of(0, 1)
            stats_of(0, 2)
            for tc in range(1, NCH):
                normed(0, tc)
                if tc + 2 < NCH:
                    stats_of(0, tc + 2)
                if tc == 1:
                    scale_bias(0)
                    gates(0)
                    ones(0)
                else:
                    split(0, tc - 2)
                if tc == NCH - 1:
                    shifts(1)
                    gates(1)
            split(0, NCH - 2)
            split(0, NCH - 1)
            for y in range(NLAY):
                attention(y)
                ffn(y)
                if y == 0:
                    ones(1)


def constants():
    bf = np.dtype("bfloat16")
    t = np.arange(T)
    i = np.arange(P)
    col = np.ones((CR, HG, T), np.float32)
    col[2], col[4] = t // 256 * 256, t % 256
    row0 = np.zeros((CR, HG, T), np.float32)
    row0[2], row0[3], row0[4], row0[5] = 1, -(t // 256 * 256), 1, -(t % 256)
    e = np.arange(NE)
    esel = np.zeros((3 * NE, RC, P), np.float32)
    for f in range(NE * FE):
        esel[f // FE::NE, f // P, f % P] = 1
    return {
        "ident": np.eye(P, dtype=np.float32), "identb": np.eye(P).astype(bf),
        "neg_m": np.where(i[None, :] > i[:, None], -1e30, 0).astype(bf),
        "neg_e": np.where(i[:, None] > i[None, :], -1e30, 0).astype(bf),
        "col_const": col.astype(bf), "row_const0": row0.astype(bf), "row_const1": np.zeros((CR, HG, T), bf),
        "tri": (e[None, :] < e[:, None]).astype(np.float32), "esel": esel.astype(bf),
    }


def laid_out(v):
    v = {k: np.asarray(x) for k, x in v.items()}

    def columns(b):
        n = -(-b.shape[0] // P)
        out = np.zeros((n * P,), b.dtype)
        out[:b.shape[0]] = b
        return np.ascontiguousarray(out.reshape(n, P).T)

    c = np.concatenate([v["L0_c"].reshape(KD, P), v["L1_c"].reshape(KD, P)]).T
    a = {
        "x": v["L0_attn_x"].reshape(T, D), "c": c, "wmod0": v["L0_wmod"], "wmod1": v["L1_wmod"],
        "w_row0": v["L0_attn_k_w"].T, "w_col0": v["L0_attn_q_w"].T, "w_v0": v["L0_attn_v_w"].T,
        "b_row0": columns(v["L0_attn_k_b"]), "b_col0": columns(v["L0_attn_q_b"]),
        "b_v0": v["L0_attn_v_b"], "b_o0": v["L0_attn_o_b"], "w_o0": v["L0_attn_o_w"].T,
        "w_row1": v["L1_attn_wq"], "w_col1": v["L1_attn_wk"], "w_v1": v["L1_attn_wv"],
        "b_row1": columns(v["L1_attn_bq"]), "b_col1": columns(v["L1_attn_bk"]),
        "b_v1": v["L1_attn_bv"], "b_o1": v["L1_attn_bo"], "w_o1": v["L1_attn_wo"],
        "w_gate0": v["L0_ffn_gate_w"].T, "w_up0": v["L0_ffn_up_w"].T, "w_down0": v["L0_ffn_down_w"].T,
        "gate_s": columns(v["L0_ffn_gate_s"]), "up_s": columns(v["L0_ffn_up_s"]), "down_s": v["L0_ffn_down_s"],
        "w_gate1": np.concatenate([v["L1_ffn_exp_wg"].reshape(NE * FE, D), v["L1_ffn_shared_wg"]]).T,
        "w_up1": np.concatenate([v["L1_ffn_exp_wu"].reshape(NE * FE, D), v["L1_ffn_shared_wu"]]).T,
        "w_down1": np.concatenate([v["L1_ffn_exp_wd"].transpose(0, 2, 1).reshape(NE * FE, D), v["L1_ffn_shared_wd"].T]),
        "gate_w": v["L1_ffn_gate_w"].T,
    }
    return {k: np.ascontiguousarray(x) for k, x in {**a, **constants()}.items()}


def kernel(**inputs):
    import concourse.bacc as bacc
    from concourse.bass_utils import run_bass_kernel_spmd

    arrays = laid_out(inputs)
    nc = bacc.Bacc("TRN2", target_bir_lowering=False, num_devices=1)
    aps = {k: nc.dram_tensor(f"in_{k}", x.shape, mybir.dt.from_np(x.dtype), kind="ExternalInput").ap()
           for k, x in arrays.items()}
    aps["out"] = nc.dram_tensor("out", (T, D), F32, kind="ExternalOutput").ap()
    adaln_two_layers(nc, aps)
    got = run_bass_kernel_spmd(nc, [{f"in_{k}": x for k, x in arrays.items()}], core_ids=[0])
    return got.results[0]["out"].reshape(1, T, D)
```
